# Optimizing a Trainium2 kernel written in Bass

```python
import numpy as np
import jax
import jax.numpy as jnp

def _softmax(x, axis=-1):
    return jax.nn.softmax(x, axis=axis)

def _gelu(x):
    return jax.nn.gelu(x, approximate=True)

def _silu(x):
    return jax.nn.silu(x)

def _sigmoid(x):
    return jax.nn.sigmoid(x)

def _layernorm(x, axis=-1, eps=1e-05):
    m = jnp.mean(x, axis=axis, keepdims=True)
    v = jnp.var(x, axis=axis, keepdims=True)
    return (x - m) / jnp.sqrt(v + eps)

def _scatter_add(tgt, idx, src, axis=0):
    return tgt.at[idx].add(src)

def _segment_sum(src, seg, n):
    return jax.ops.segment_sum(src, seg, n)
kernel_name = 'mk_flamingo_gated_d2_seqx_r4_3dc5e5'

def setup_inputs(seed: int=0):
    np.random.seed(seed)
    _w = jnp.asarray

    def _rec_inputs():
        import jax
        import jax.numpy as jnp
        _rk = jax.random.key(seed)
        x = -0.0003929 + 0.9999 * jax.random.normal(jax.random.fold_in(_rk, 1), (8, 256, 512), jnp.float32)
        _lenS = 256 - jax.random.randint(jax.random.fold_in(_rk, 7), (8,), 0, max(1, 256 // 4) + 1, jnp.int32)
        _lenS2 = 256 - jax.random.randint(jax.random.fold_in(_rk, 8), (8,), 0, max(1, 256 // 4) + 1, jnp.int32)
        _ctx_2048P = jax.random.normal(jax.random.fold_in(_rk, 11), (8, 16, 512), jnp.float32)
        _ctx_2048c = jax.random.dirichlet(jax.random.fold_in(_rk, 511), 0.3 * jnp.ones((16,), jnp.float32), (8, 256))
        _ctx_2048t = jnp.einsum('bsk,bkd->bsd', _ctx_2048c, _ctx_2048P)
        _ctx_2048t = _ctx_2048t * jax.lax.rsqrt(jnp.mean(jnp.square(_ctx_2048t)) + 1e-12) * 0.953939
        ctx_2048 = 2.81802e-05 + 1.00001 * (_ctx_2048t + 0.3 * jax.random.normal(jax.random.fold_in(_rk, 611), (8, 256, 512), jnp.float32))
        _g = jax.random.normal(jax.random.fold_in(_rk, 9001), (2, 2), jnp.float32)
        _g = jnp.sign(_g) * jnp.maximum(jnp.abs(_g), 1.0) + (_g == 0) * 1.0
        g_xattn = _g[0]
        g_ffn = _g[1]
        return (x, ctx_2048, _lenS2, g_xattn, g_ffn)
    x, ctx_2048, _lenS2, g_xattn, g_ffn = _rec_inputs()

    def _L0_xattn_setup():
        import jax, jax.numpy as jnp
        import numpy as np
        HIDDEN = 512
        NUM_HEADS = 16
        HEAD_DIM = HIDDEN // NUM_HEADS
        CHUNK = 256
        SCALE = HEAD_DIM ** (-0.5)

        def _chunked_causal_attention(q, k, v):
            B, H, S, D = q.shape
            n_chunks = S // CHUNK
            kc = k.reshape(B, H, n_chunks, CHUNK, D).transpose(2, 0, 1, 3, 4)
            vc = v.reshape(B, H, n_chunks, CHUNK, D).transpose(2, 0, 1, 3, 4)
            j0s = jnp.arange(n_chunks) * CHUNK
            q_idx = jnp.arange(S)[:, None]
            k_off = jnp.arange(CHUNK)[None, :]
            out0 = jnp.zeros_like(q)
            m0 = jnp.full((B, H, S, 1), -jnp.inf, dtype=q.dtype)
            s0 = jnp.zeros((B, H, S, 1), dtype=q.dtype)

            def step(carry, inputs):
                out, m, s = carry
                kj, vj, j0 = inputs
                scores = jnp.einsum('bhqd,bhkd->bhqk', q, kj) * SCALE
                causal = j0 + k_off > q_idx
                scores = jnp.where(causal[None, None], -jnp.inf, scores)
                chunk_max = scores.max(axis=-1, keepdims=True)
                new_m = jnp.maximum(m, chunk_max)
                exp_old = jnp.exp(m - new_m)
                exp_c = jnp.exp(scores - new_m)
                new_s = s * exp_old + exp_c.sum(axis=-1, keepdims=True)
                out = out * (s / new_s) * exp_old + jnp.einsum('bhqk,bhkd->bhqd', exp_c / new_s, vj)
                return ((out, new_m, new_s), None)
            (out, _, _), _ = jax.lax.scan(step, (out0, m0, s0), (kc, vc, j0s))
            return out
        key = jax.random.key(seed)
        kq, kk, kv = jax.random.split(key, 3)
        B, S = (2, 1024)
        return {'query': jax.random.normal(kq, (B, S, HIDDEN), dtype=jnp.float32), 'key': jax.random.normal(kk, (B, S, HIDDEN), dtype=jnp.float32), 'value': jax.random.normal(kv, (B, S, HIDDEN), dtype=jnp.float32)}
    _L0_xattn_all = _L0_xattn_setup()
    _L0_xattn_in = {k: v for k, v in _L0_xattn_all.items() if k in ()}
    del _L0_xattn_all

    def _L0_ffn_setup():
        import jax, jax.numpy as jnp
        import numpy as np
        HIDDEN = 512
        INTER = 192
        N_EXPERTS = 32
        TOP_K = 8
        key = jax.random.key(seed)
        k = jax.random.split(key, 5)
        s = 1.0 / np.sqrt(HIDDEN)
        return {'hidden_states': jax.random.normal(k[0], (1, 256, HIDDEN), jnp.float32), 'gate_w': jax.random.normal(k[1], (HIDDEN, N_EXPERTS), jnp.float32) * s, 'w_gate': jax.random.normal(k[2], (N_EXPERTS, HIDDEN, INTER), jnp.float32) * s, 'w_up': jax.random.normal(k[3], (N_EXPERTS, HIDDEN, INTER), jnp.float32) * s, 'w_down': jax.random.normal(k[4], (N_EXPERTS, INTER, HIDDEN), jnp.float32) * (1.0 / np.sqrt(INTER))}
    _L0_ffn_all = _L0_ffn_setup()
    _L0_ffn_in = {k: v for k, v in _L0_ffn_all.items() if k in ('gate_w', 'w_gate', 'w_up', 'w_down')}
    del _L0_ffn_all

    def _L1_xattn_setup():
        import jax, jax.numpy as jnp
        import numpy as np
        DIM = 512
        HEADS = 16
        HEAD_DIM = DIM // HEADS
        EPS = 1e-06
        IMG_TOKENS = 257
        B, L1, L2 = (2, 1024, 769)
        SCALE = 1.0 / np.sqrt(HEAD_DIM).astype(np.float32)

        def rms_norm(x, g):
            return x * jax.lax.rsqrt(jnp.mean(x * x, axis=-1, keepdims=True) + EPS) * g

        def attention(q, k, v, kv_mask=None):
            s = jnp.einsum('bqhd,bkhd->bhqk', q, k) * SCALE
            if kv_mask is not None:
                s = jnp.where(kv_mask[:, None, None, :], s, jnp.float32(-1000000000.0))
            p = jax.nn.softmax(s, axis=-1)
            return jnp.einsum('bhqk,bkhd->bqhd', p, v)
        key = jax.random.key(seed)
        ks = jax.random.split(key, 20)
        std = 0.02

        def lin(i):
            return (jax.random.normal(ks[i], (DIM, DIM), jnp.float32) * std, jnp.zeros((DIM,), jnp.float32))
        w_q, b_q = lin(0)
        w_k, b_k = lin(1)
        w_v, b_v = lin(2)
        w_k_img, b_k_img = lin(3)
        w_v_img, b_v_img = lin(4)
        w_o, b_o = lin(5)
        return {'x': jax.random.normal(ks[6], (B, L1, DIM), jnp.float32), 'context': jax.random.normal(ks[7], (B, L2, DIM), jnp.float32), 'context_lens': jax.random.randint(ks[8], (B,), 64, 513, jnp.int64 if jax.config.jax_enable_x64 else jnp.int32), 'w_q': w_q, 'b_q': b_q, 'w_k': w_k, 'b_k': b_k, 'w_v': w_v, 'b_v': b_v, 'w_k_img': w_k_img, 'b_k_img': b_k_img, 'w_v_img': w_v_img, 'b_v_img': b_v_img, 'w_o': w_o, 'b_o': b_o, 'g_q': jnp.ones((DIM,), jnp.float32), 'g_k': jnp.ones((DIM,), jnp.float32), 'g_k_img': jnp.ones((DIM,), jnp.float32)}
    _L1_xattn_all = _L1_xattn_setup()
    _L1_xattn_in = {k: v for k, v in _L1_xattn_all.items() if k in ('w_q', 'b_q', 'w_k', 'b_k', 'w_v', 'b_v', 'w_k_img', 'b_k_img', 'w_v_img', 'b_v_img', 'w_o', 'b_o', 'g_q', 'g_k', 'g_k_img')}
    del _L1_xattn_all

    def _L1_ffn_setup():
        import jax, jax.numpy as jnp
        import numpy as np
        B, S, D_IN, D_OUT = (4, 512, 512, 512)
        EPS = 1e-10
        key = jax.random.key(seed)
        kx, kw, kb = jax.random.split(key, 3)
        x = jax.random.normal(kx, (B, S, D_IN), dtype=jnp.float32)
        weight = jax.random.normal(kw, (D_OUT, D_IN), dtype=jnp.float32) * 0.02
        bias = jax.random.normal(kb, (D_OUT,), dtype=jnp.float32) * 0.02
        return {'x': x, 'weight': weight, 'bias': bias}
    _L1_ffn_all = _L1_ffn_setup()
    _L1_ffn_in = {k: v for k, v in _L1_ffn_all.items() if k in ('weight', 'bias')}
    del _L1_ffn_all
    return {'x': x, 'ctx_2048': ctx_2048, '_lenS2': _lenS2, 'g_xattn': g_xattn, 'g_ffn': g_ffn, 'L0_ffn_gate_w': _L0_ffn_in['gate_w'], 'L0_ffn_w_gate': _L0_ffn_in['w_gate'], 'L0_ffn_w_up': _L0_ffn_in['w_up'], 'L0_ffn_w_down': _L0_ffn_in['w_down'], 'L1_xattn_w_q': _L1_xattn_in['w_q'], 'L1_xattn_b_q': _L1_xattn_in['b_q'], 'L1_xattn_w_k': _L1_xattn_in['w_k'], 'L1_xattn_b_k': _L1_xattn_in['b_k'], 'L1_xattn_w_v': _L1_xattn_in['w_v'], 'L1_xattn_b_v': _L1_xattn_in['b_v'], 'L1_xattn_w_k_img': _L1_xattn_in['w_k_img'], 'L1_xattn_b_k_img': _L1_xattn_in['b_k_img'], 'L1_xattn_w_v_img': _L1_xattn_in['w_v_img'], 'L1_xattn_b_v_img': _L1_xattn_in['b_v_img'], 'L1_xattn_w_o': _L1_xattn_in['w_o'], 'L1_xattn_b_o': _L1_xattn_in['b_o'], 'L1_xattn_g_q': _L1_xattn_in['g_q'], 'L1_xattn_g_k': _L1_xattn_in['g_k'], 'L1_xattn_g_k_img': _L1_xattn_in['g_k_img'], 'L1_ffn_weight': _L1_ffn_in['weight'], 'L1_ffn_bias': _L1_ffn_in['bias']}

def reference(x, ctx_2048, _lenS2, g_xattn, g_ffn, L0_ffn_gate_w, L0_ffn_w_gate, L0_ffn_w_up, L0_ffn_w_down, L1_xattn_w_q, L1_xattn_b_q, L1_xattn_w_k, L1_xattn_b_k, L1_xattn_w_v, L1_xattn_b_v, L1_xattn_w_k_img, L1_xattn_b_k_img, L1_xattn_w_v_img, L1_xattn_b_v_img, L1_xattn_w_o, L1_xattn_b_o, L1_xattn_g_q, L1_xattn_g_k, L1_xattn_g_k_img, L1_ffn_weight, L1_ffn_bias):
    import jax
    import jax.numpy as jnp

    def _L0_xattn_ref(query, key, value):
        import jax, jax.numpy as jnp
        import numpy as np
        HIDDEN = 512
        NUM_HEADS = 16
        HEAD_DIM = HIDDEN // NUM_HEADS
        CHUNK = 256
        SCALE = HEAD_DIM ** (-0.5)

        def _chunked_causal_attention(q, k, v):
            B, H, S, D = q.shape
            n_chunks = S // CHUNK
            kc = k.reshape(B, H, n_chunks, CHUNK, D).transpose(2, 0, 1, 3, 4)
            vc = v.reshape(B, H, n_chunks, CHUNK, D).transpose(2, 0, 1, 3, 4)
            j0s = jnp.arange(n_chunks) * CHUNK
            q_idx = jnp.arange(S)[:, None]
            k_off = jnp.arange(CHUNK)[None, :]
            out0 = jnp.zeros_like(q)
            m0 = jnp.full((B, H, S, 1), -jnp.inf, dtype=q.dtype)
            s0 = jnp.zeros((B, H, S, 1), dtype=q.dtype)

            def step(carry, inputs):
                out, m, s = carry
                kj, vj, j0 = inputs
                scores = jnp.einsum('bhqd,bhkd->bhqk', q, kj) * SCALE
                causal = j0 + k_off > q_idx
                scores = jnp.where(causal[None, None], -jnp.inf, scores)
                chunk_max = scores.max(axis=-1, keepdims=True)
                new_m = jnp.maximum(m, chunk_max)
                exp_old = jnp.exp(m - new_m)
                exp_c = jnp.exp(scores - new_m)
                new_s = s * exp_old + exp_c.sum(axis=-1, keepdims=True)
                out = out * (s / new_s) * exp_old + jnp.einsum('bhqk,bhkd->bhqd', exp_c / new_s, vj)
                return ((out, new_m, new_s), None)
            (out, _, _), _ = jax.lax.scan(step, (out0, m0, s0), (kc, vc, j0s))
            return out
        B, S, _ = query.shape
        q = query.reshape(B, S, NUM_HEADS, HEAD_DIM).transpose(0, 2, 1, 3)
        k = key.reshape(B, S, NUM_HEADS, HEAD_DIM).transpose(0, 2, 1, 3)
        v = value.reshape(B, S, NUM_HEADS, HEAD_DIM).transpose(0, 2, 1, 3)
        out = _chunked_causal_attention(q, k, v)
        return out.transpose(0, 2, 1, 3).reshape(B, S, HIDDEN)

    def _L0_ffn_ref(hidden_states, gate_w, w_gate, w_up, w_down):
        import jax, jax.numpy as jnp
        import numpy as np
        HIDDEN = 512
        INTER = 192
        N_EXPERTS = 32
        TOP_K = 8
        B, S, H = hidden_states.shape
        E = gate_w.shape[1]
        x = hidden_states.reshape(-1, H)
        T = x.shape[0]
        K = TOP_K
        P = T * K
        C = 2 * (P // E)
        probs = jax.nn.softmax(x @ gate_w, axis=-1)
        w, sel = jax.lax.top_k(probs, K)
        w = w / jnp.sum(w, axis=-1, keepdims=True)
        flat_e = sel.reshape(-1)
        flat_t = jnp.repeat(jnp.arange(T), K)
        flat_w = w.reshape(-1)
        order = jnp.argsort(flat_e)
        se = flat_e[order]
        start = jnp.searchsorted(se, jnp.arange(E))
        pos = jnp.arange(P) - start[se]
        slot = jnp.where(pos < C, se * C + pos, E * C)
        slot_pair = jnp.full((E * C,), P, dtype=jnp.int32).at[slot].set(order.astype(jnp.int32), mode='drop')
        t_slot = jnp.concatenate([flat_t, jnp.array([T])])[slot_pair]
        w_slot = jnp.concatenate([flat_w, jnp.zeros((1,), flat_w.dtype)])[slot_pair]
        x_pad = jnp.concatenate([x, jnp.zeros((1, H), x.dtype)], axis=0)
        xg = x_pad[t_slot].reshape(E, C, H)
        g = jnp.einsum('ech,ehi->eci', xg, w_gate)
        u = jnp.einsum('ech,ehi->eci', xg, w_up)
        y = jnp.einsum('eci,eih->ech', jax.nn.silu(g) * u, w_down).reshape(E * C, H)
        out = jnp.zeros((T + 1, H), x.dtype).at[t_slot].add(w_slot[:, None] * y)
        return out[:T].reshape(B, S, H)

    def _L1_xattn_ref(x, context, context_lens, w_q, b_q, w_k, b_k, w_v, b_v, w_k_img, b_k_img, w_v_img, b_v_img, w_o, b_o, g_q, g_k, g_k_img):
        import jax, jax.numpy as jnp
        import numpy as np
        DIM = 512
        HEADS = 16
        HEAD_DIM = DIM // HEADS
        EPS = 1e-06
        IMG_TOKENS = 257
        B, L1, L2 = (2, 1024, 769)
        SCALE = 1.0 / np.sqrt(HEAD_DIM).astype(np.float32)

        def rms_norm(x, g):
            return x * jax.lax.rsqrt(jnp.mean(x * x, axis=-1, keepdims=True) + EPS) * g

        def attention(q, k, v, kv_mask=None):
            s = jnp.einsum('bqhd,bkhd->bhqk', q, k) * SCALE
            if kv_mask is not None:
                s = jnp.where(kv_mask[:, None, None, :], s, jnp.float32(-1000000000.0))
            p = jax.nn.softmax(s, axis=-1)
            return jnp.einsum('bhqk,bkhd->bqhd', p, v)
        b = x.shape[0]
        ctx_img = context[:, :IMG_TOKENS]
        ctx_txt = context[:, IMG_TOKENS:]
        q = rms_norm(x @ w_q.T + b_q, g_q).reshape(b, -1, HEADS, HEAD_DIM)
        k = rms_norm(ctx_txt @ w_k.T + b_k, g_k).reshape(b, -1, HEADS, HEAD_DIM)
        v = (ctx_txt @ w_v.T + b_v).reshape(b, -1, HEADS, HEAD_DIM)
        k_img = rms_norm(ctx_img @ w_k_img.T + b_k_img, g_k_img).reshape(b, -1, HEADS, HEAD_DIM)
        v_img = (ctx_img @ w_v_img.T + b_v_img).reshape(b, -1, HEADS, HEAD_DIM)
        txt_len = ctx_txt.shape[1]
        kv_mask = jnp.arange(txt_len)[None, :] < context_lens[:, None]
        img_x = attention(q, k_img, v_img)
        txt_x = attention(q, k, v, kv_mask)
        out = (txt_x + img_x).reshape(b, -1, DIM)
        return out @ w_o.T + b_o

    def _L1_ffn_ref(x, weight, bias):
        import jax, jax.numpy as jnp
        import numpy as np
        B, S, D_IN, D_OUT = (4, 512, 512, 512)
        EPS = 1e-10
        scale = jnp.mean(jnp.abs(weight))
        w_t = jnp.clip(jnp.round(weight / (scale + EPS)), -1.0, 1.0)
        w_ste = weight + jax.lax.stop_gradient(w_t * scale - weight)
        return jnp.einsum('bsi,oi->bso', x, w_ste) + bias
    x = x + jnp.tanh(g_xattn[0]) * _L0_xattn_ref(_layernorm(x, axis=-1), ctx_2048, ctx_2048)
    x = x + jnp.tanh(g_ffn[0]) * _L0_ffn_ref(_layernorm(x, axis=-1), L0_ffn_gate_w, L0_ffn_w_gate, L0_ffn_w_up, L0_ffn_w_down)
    x = x + jnp.tanh(g_xattn[1]) * _L1_xattn_ref(_layernorm(x, axis=-1), ctx_2048, _lenS2, L1_xattn_w_q, L1_xattn_b_q, L1_xattn_w_k, L1_xattn_b_k, L1_xattn_w_v, L1_xattn_b_v, L1_xattn_w_k_img, L1_xattn_b_k_img, L1_xattn_w_v_img, L1_xattn_b_v_img, L1_xattn_w_o, L1_xattn_b_o, L1_xattn_g_q, L1_xattn_g_k, L1_xattn_g_k_img)
    x = x + jnp.tanh(g_ffn[1]) * _L1_ffn_ref(_layernorm(x, axis=-1), L1_ffn_weight, L1_ffn_bias)
    return x

_drawn_inputs = setup_inputs


def setup_inputs(seed=0):
    import zlib

    import numpy as np

    out = dict(_drawn_inputs(seed))
    spreads = {'g_ffn': (-1.0, 0.6),
     'L1_xattn_b_q': (0.0, 2.0),
     'L1_xattn_b_k': (0.0, 0.1),
     'L1_xattn_b_v': (0.0, 0.1),
     'L1_xattn_b_k_img': (0.0, 2.0),
     'L1_xattn_b_v_img': (0.0, 0.1),
     'L1_xattn_b_o': (0.0, 0.1),
     'L1_xattn_g_q': (1.0, 0.6),
     'L1_xattn_g_k': (1.0, 0.2),
     'L1_xattn_g_k_img': (1.0, 0.6)}
    factors = {'L1_ffn_bias': 4.246, 'L1_xattn_w_q': 24.884, 'L1_xattn_w_k_img': 4.957}
    for name, (base, spread) in spreads.items():
        noise = np.random.default_rng([zlib.crc32(name.encode()), seed]).standard_normal(out[name].shape)
        drawn = base * np.exp(spread * noise) if base else spread * noise
        out[name] = jnp.asarray(drawn.astype(out[name].dtype))
    for name, factor in factors.items():
        out[name] = (out[name] * factor).astype(out[name].dtype)
    return out
```

```python
import numpy as np

from contextlib import ExitStack

import concourse.bass as bass
from concourse import mybir

F32 = mybir.dt.float32
F16 = mybir.dt.float16
BF16 = mybir.dt.bfloat16
I32 = mybir.dt.int32
ALU = mybir.AluOpType
ACT = mybir.ActivationFunctionType
AX = mybir.AxisListType.X

P = 128
B, S, H = 8, 256, 512
T = B * S
QT = S // P
HC = H // P
NH, D = 16, 32
E, FI, TOPK = 32, 192, 8
CAP = 2 * (T * TOPK // E)
TPE = CAP // P
MT = T * TOPK // P + E
ROW = H + E
GU = 2 * FI
WEXP = HC * GU + 2 * H
NW, NY = 3, 4
LN_EPS, RMS_EPS, TERN_EPS = 1e-5, 1e-6, 1e-10
MASKED = -1e30
FAR = float(1 << 20)

SC_N = 2.0**10
SC_C = 2.0**8
SC_W = 2.0**8
SC_Q, SC_K = 2.0**4, 2.0**11
SC_H = 2.0**6
SC_A = 2.0**8

ROUND = 1.5 * 2.0**23

STEPS = QT * NH // 2


class Chain:

    def __init__(self, eng, sem, per_batch):
        self.eng, self.sem, self.per = eng, sem, per_batch
        self.base, self.n = 0, 0

    def batch(self, b):
        self.base, self.n = b * self.per, 0

    def mark(self, ins):
        ins.then_inc(self.sem, 1)
        self.n += 1

    def settle(self):
        self.eng.wait_ge(self.sem, self.base + self.n)

    def link(self, ins):
        self.mark(ins)
        self.settle()

    def end(self, name):
        assert self.n == self.per, (name, self.n, self.per)


def broadcast_rows(ap, n):
    return bass.AP(ap.tensor, ap.offset, [[0, n], [1, ap.shape[-1]]])


def rep(ap, n, at):
    dims = [list(d) for d in ap.ap]
    dims.insert(at, [0, n])
    return bass.AP(ap.tensor, ap.offset, dims)


class Batch:

    def __init__(self, n, par, half):
        self.n, self.par, self.half = n, par, half

    def next(self):
        return Batch(self.n + 1, 1 - self.par, self.half + self.par)

    def prev(self):
        return Batch(self.n - 1, 1 - self.par, self.half - (1 - self.par))


def over_batches(eng, first, body, last):
    first(Batch(0, 0, 0))
    with eng.Fori(0, (B - 2) // 2) as i:
        body(Batch(2 * i + 1, 1, i))
        body(Batch(2 * i + 2, 0, i + 1))
    last(Batch(B - 1, 1, (B - 1) // 2))


class Attention:

    def __init__(self, nc, sb, sem, bank, tag, causal, scale, v, id32, id16, idb, maskb):
        self.nc, self.causal, self.scale, self.v = nc, causal, scale, v
        self.id32, self.id16, self.idb, self.maskb = id32, id16, idb, maskb
        self.pS, self.pT, self.pO, self.bank = bank[0:2], bank[2:4], bank[4], bank[5]
        self.parts = sb(tag + "parts", [P, 2 * QT, NH, 4, D], F16)
        self.stack = sb(tag + "stack", [P, 2, 2, NH, S], F16)
        self.nmax = sb(tag + "nmax", [P, 4, 2])
        self.bias = sb(tag + "bias", [P, 4, 2])
        self.probs = sb(tag + "probs", [P, 2, 2, S])
        self.probsT = sb(tag + "probsT", [P, 2, 4 * P])
        self.sums = sb(tag + "sums", [P, 2, QT, NH])
        self.outT = sb(tag + "outT", [P, 2, QT, H])
        self.hi_ready, self.parts_ready = sem(tag + "hi_ready"), sem(tag + "parts_ready")
        self.stack_ps, self.stack_ready = sem(tag + "stack_ps"), sem(tag + "stack_ready")
        self.scores_made, self.max_made, self.bias_made = sem(tag + "scores"), sem(tag + "max"), sem(tag + "bias_s")
        self.probs_made, self.turned, self.probsT_made = sem(tag + "probs_s"), sem(tag + "turned"), sem(tag + "probsT_s")
        self.out_made, self.out_read = sem(tag + "out_made"), sem(tag + "out_read")

    def nk_of(self, s):
        return P if self.causal and s < STEPS // 2 else S

    def pe_scores(self, b, s):
        qt, nk = s // (STEPS // 2), self.nk_of(s)
        for u in range(2):
            h = 2 * (s % (STEPS // 2)) + u
            o = self.pS[s % 2][:, u * S : u * S + nk]
            last = self.nc.tensor.matmul(o, self.stack[:, b.par, 0, h, qt * P : (qt + 1) * P],
                                    self.stack[:, b.par, 1, h, 0:nk], start=True, stop=not self.causal)
            if self.causal:
                last = self.nc.tensor.matmul(self.pS[s % 2][:, u * S + qt * P : u * S + (qt + 1) * P], self.idb[:], self.maskb[:],
                                        start=False, stop=True)
        last.then_inc(self.scores_made, 1)

    def pe_pv(self, pe, b, s):
        qt, j = s // (STEPS // 2), s % (STEPS // 2)
        nkt = self.nk_of(s) // P
        pe.wait_ge(self.probsT_made, STEPS * b.n + s + 1)
        if j == 0:
            pe.wait_ge(self.out_read, 2 * b.n + qt + 1)
        for u in range(2):
            h = 2 * j + u
            r, g = h % 4, h // 4
            for kt in range(nkt):
                last = self.nc.tensor.matmul(self.pO[D * r : D * r + D, g * P : (g + 1) * P], self.v[:, b.par, kt, D * h : D * h + D],
                                        self.probsT[:, s % 2, (2 * kt + u) * P : (2 * kt + u + 1) * P],
                                        start=kt == 0, stop=kt == nkt - 1)
        if j == STEPS // 2 - 1:
            last.then_inc(self.out_made, 1)

    def pe_step(self, pe, b, s, more, before=True):
        nkt = self.nk_of(s) // P
        pe.wait_ge(self.probs_made, STEPS * b.n + s + 1)
        if s + 2 < STEPS:
            self.pe_scores(b, s + 2)
        elif more:
            if s + 2 == STEPS:
                pe.wait_ge(self.stack_ready, 8 * b.next().n + 9)
            self.pe_scores(b.next(), s + 2 - STEPS)
        for kt in range(nkt):
            for u in range(2):
                last = self.nc.tensor.transpose(self.pT[s % 2][:, (2 * kt + u) * P : (2 * kt + u + 1) * P],
                                           self.probs[:, s % 2, u, kt * P : (kt + 1) * P], self.id32[:])
        last.then_inc(self.turned, 1)
        if s > 0:
            self.pe_pv(pe, b, s - 1)
        elif before:
            self.pe_pv(pe, b.prev(), STEPS - 1)

    def act_exp(self, act, b, s):
        qt, nk = s // (STEPS // 2), self.nk_of(s)
        act.wait_ge(self.bias_made, STEPS * b.n + s + 1)
        for u in range(2):
            h = 2 * (s % (STEPS // 2)) + u
            last = self.nc.scalar.activation(self.probs[:, s % 2, u, 0:nk], self.pS[s % 2][:, u * S : u * S + nk], ACT.Exp,
                                        bias=self.bias[:, s % 4, u : u + 1], scale=self.scale,
                                        accum_out=self.sums[:, b.par, qt, h : h + 1])
        last.then_inc(self.probs_made, 1)

    def act_step(self, act, b, s, more):
        if s + 1 < STEPS:
            self.act_exp(act, b, s + 1)
        elif more:
            self.act_exp(act, b.next(), 0)
        w = self.nk_of(s) // P * 2 * P
        act.wait_ge(self.turned, STEPS * b.n + s + 1)
        self.nc.scalar.activation(self.probsT[:, s % 2, 0:w], self.pT[s % 2][:, 0:w], ACT.Copy).then_inc(self.probsT_made, 1)

    def dve_max(self, dve, b, s):
        nk = self.nk_of(s)
        dve.wait_ge(self.scores_made, STEPS * b.n + s + 1)
        v = self.pS[s % 2][:, :].rearrange("p (u k) -> p u k", u=2)[:, :, 0:nk]
        self.nc.vector.tensor_reduce(self.nmax[:, s % 4, :], v, AX, ALU.max).then_inc(self.max_made, 1)
        dve.wait_ge(self.max_made, STEPS * b.n + s + 1)
        self.nc.vector.tensor_scalar(self.bias[:, s % 4, :], self.nmax[:, s % 4, :], -self.scale, None, ALU.mult).then_inc(self.bias_made, 1)

    def dve_step(self, dve, b, s, more, before=True):
        if s + 2 < STEPS:
            self.dve_max(dve, b, s + 2)
        elif more:
            self.dve_max(dve, b.next(), s + 2 - STEPS)
        if s == STEPS // 2:
            self.dve_out(dve, b, 0)
        if s == 0 and before:
            self.dve_out(dve, b.prev(), 1)

    def dve_out(self, dve, b, t):
        dve.wait_ge(self.out_made, 2 * b.n + t + 1)
        self.nc.vector.tensor_copy(self.outT[:, b.par, t, :], self.pO[:, :]).then_inc(self.out_read, 1)

    def part(self, j, which):
        return self.parts[:, j, :, which * (2 if j < QT else 1), :]

    def act_hi(self, act, b, j, src, scale):
        act.wait_ge(self.stack_ps, 8 * b.n + 2 * j + 2)
        self.nc.scalar.activation(self.part(j, 0), src.rearrange("p (h d) -> p h d", d=D), ACT.Copy, scale=scale)\
          .then_inc(self.hi_ready, 1)

    def dve_lo(self, dve, b, j, src, scale, chain):
        dve.wait_ge(self.hi_ready, 4 * b.n + j + 1)
        chain.link(self.nc.vector.scalar_tensor_tensor(self.part(j, 1), src.rearrange("p (h d) -> p h d", d=D), scale,
                                                  self.part(j, 0), ALU.mult, ALU.subtract))
        if j < QT:
            o, i = self.parts[:, j, :, 1:4:2, :], self.parts[:, j, :, 0:4:2, :]
        else:
            o, i = self.parts[:, j, :, 2:4, :], self.parts[:, j, :, 0:2, :]
        self.nc.vector.tensor_copy(o, i).then_inc(self.parts_ready, 1)

    def pe_stack(self, pe, b, k):
        j = k // 2
        pe.wait_ge(self.parts_ready, 4 * b.n + j + 1)
        pe.wait_ge(self.stack_ready, 8 * b.n + k + 1)
        o = self.bank[:, :].bitcast(F16)
        for u in range(8):
            last = self.nc.tensor.transpose(o[:, u * P : (u + 1) * P],
                                       self.parts[:, j, 8 * (k % 2) + u, :, :].rearrange("p a d -> p (a d)"), self.id16[:])
        last.then_inc(self.stack_ps, 1)

    def dve_stack(self, dve, b, k):
        j = k // 2
        dve.wait_ge(self.stack_ps, 8 * b.n + k + 9)
        self.nc.vector.tensor_copy(self.stack[:, b.par, j // QT, 8 * (k % 2) : 8 * (k % 2) + 8, (j % QT) * P : (j % QT + 1) * P],
                              self.bank[:, :].bitcast(F16).rearrange("p (h q) -> p h q", h=8)).then_inc(self.stack_ready, 1)


class Shared:

    def __init__(self, nc, es):
        def sb(name, shape, dt=F32):
            return es.enter_context(nc.sbuf_tensor(name, shape, dt))

        def dram(name, shape, dt=F32):
            return nc.dram_tensor(name, shape, dt, kind="Internal").ap()

        self.tokens = dram("tokens", (T + P, ROW))
        self.slots = dram("slots", (E * CAP, 1))
        self.acc = [dram(f"acc{i}", (T + P, H)) for i in range(2)]
        self.id32 = sb("id32", [P, P])
        self.id16 = sb("id16", [P, P], F16)
        self.tri = sb("tri", [P, P], F16)
        self.shift = sb("shift", [E, 2, E], F16)
        self.ones = sb("ones", [P, P], F16)
        self.ones32 = sb("ones32", [P, P])
        self.neghalf = sb("neghalf", [P, 4])
        self.token_ids = sb("token_ids", [P, T // P + 1])
        self.thr = sb("thr", [E, TPE - 1])
        self.tiles_iota = sb("tiles_iota", [E, MT])
        self.gates = sb("gates", [P, 4])
        self.xs = sb("xs", [P, T // P, H])
        self.cum = sb("cum", [P, QT + 1, E], F16)
        self.bank = [es.enter_context(nc.psum_tensor(f"bank{i}", [P, 512], F32)) for i in range(8)]


def layer0(nc, shared, x, ctx, g_xattn, g_ffn, gate_w):
    es = ExitStack()
    with es:

        def sb(name, shape, dt=F32):
            return es.enter_context(nc.sbuf_tensor(name, shape, dt))

        def sem(name):
            return es.enter_context(nc.semaphore(name))

        def sems(name, n):
            return [sem(f"{name}{i}") for i in range(n)]

        tokens, slots, acc, xs, cum, bank = shared.tokens, shared.slots, shared.acc, shared.xs, shared.cum, shared.bank
        id32, id16, tri, shift, ones, neghalf = shared.id32, shared.id16, shared.tri, shared.shift, shared.ones, shared.neghalf
        token_ids, thr, tiles_iota, gates = shared.token_ids, shared.thr, shared.tiles_iota, shared.gates

        idb = sb("idb", [P, P], BF16)
        maskb = sb("maskb", [P, P], BF16)
        eoff = sb("eoff", [P, E])
        pads = sb("pads", [P, P])
        zeros = sb("zeros", [P, ROW])
        gates_in = sb("gates_in", [P, 4])
        gw = sb("gw", [P, HC, E])

        cbuf = sb("cbuf", [P, 2, QT, H])
        mv = sb("mv", [P, 2, QT, 2])
        st6 = sb("st6", [P, 2, QT, 6])
        rstd = sb("rstd", [P, 2, QT])
        xn = sb("xn", [P, QT, H])
        rsum = sb("rsum", [P, QT, NH])
        att = sb("att", [P, H])

        xe = sb("xe", [P, 2, QT, ROW])
        xeT = sb("xeT", [P, QT, H])
        lg = sb("lg", [P, QT, E])
        top = sb("top", [P, QT, TOPK])
        rp = sb("rp", [P, QT, E])
        lgm = sb("lgm", [P, QT, E])
        ex = sb("ex", [P, QT, E])
        chosen = sb("chosen", [P, QT, E])
        chosen16 = sb("chosen16", [P, QT, E], F16)
        ws = sb("ws", [P, QT])
        slot1 = sb("slot1", [P, QT, E])
        kept = sb("kept", [P, QT, E])
        key = sb("key", [P, QT, E])
        k8 = sb("k8", [P, QT, TOPK])
        far = sb("far", [P, QT, TOPK])
        slot_ix = sb("slot_ix", [P, 2, QT, TOPK], I32)
        tok = sb("tok", [P, 2, QT])

        mPost = bank[6]
        SCALE0 = D**-0.5 / (SC_N * SC_C)
        at = Attention(nc, sb, sem, bank, "l0_", True, SCALE0, cbuf, id32, id16, idb, maskb)

        consts = sem("consts")
        c_in = sem("c_in")
        gates_ready = sem("gates_ready")
        zero_in = sem("zero_in")
        x_loaded, c_loaded = sems("x_loaded", 2), sems("c_loaded", 2)
        x_var, x_rstd, xn_ready = sem("x_var"), sem("x_rstd"), sem("xn_ready")
        post_ps, post_read = sem("post_ps"), sem("post_read")
        p_var, p_rstd, xe_norm = sem("p_var"), sem("p_rstd"), sem("xe_norm")
        gate_shift, gate_exp, chosen_r = sem("gate_shift"), sem("gate_exp"), sem("chosen_r")
        xe_full, xe_free, xe_stored = sem("xe_full"), sem("xe_free"), sems("xe_stored", 2)
        slots_ready, slots_free, slots_sent = sem("slots_ready"), sem("slots_free"), sems("slots_sent", 2)
        dve_prep, dve_post, pool_prep, pool_post = sem("dve_prep"), sem("dve_post"), sem("pool_prep"), sem("pool_post")
        start_dve = sem("start_dve")
        dve_held = sem("dve_held")

        block = es.enter_context(nc.Block())
        N_CONST = 22

        PREP0 = {4: ["ln"], 6: ["xn"], 7: ["c"], 8: [0], 9: [1, 2], 10: [3], 11: [4, 5], 12: [6], 13: [7]}
        POST0 = {1: ["o0"], 2: ["o1"], 3: ["n"], 4: ["x0"], 5: ["x1"], 6: ["g"], 7: ["r1"], 8: ["pos"], 9: ["r2"]}
        SENDS = {9: 2, 10: 2, 11: 2, 12: 2, 13: 2, 14: 3, 15: 3}
        M_POST = 6

        def pe_prep0(pe, b, piece):
            if not isinstance(piece, str):
                at.pe_stack(pe, b, piece)

        def act_prep0(act, b, piece):
            if piece == "xn":
                for t in range(QT):
                    act.wait_ge(xn_ready, QT * b.n + t + 1)
                    at.act_hi(act, b, t, xn[:, t, :], SC_N)
            if piece == "c":
                act.wait_ge(c_loaded[b.par], 16 * b.half + 16)
                for t in range(QT):
                    at.act_hi(act, b, QT + t, cbuf[:, b.par, t, :], SC_C)

        def pool_prep0(pool, b, piece):
            if piece == "ln":
                pool.wait_ge(x_var, b.n + 1)
                nc.gpsimd.tensor_tensor(rstd[:, 0, :], mv[:, 0, :, 1], neghalf[:, 0:QT], ALU.pow).then_inc(x_rstd, 1)

        K_PREP0 = 2 * QT + 2 * QT

        def dve_prep0(dve, b, piece, chain):
            if piece == "ln":
                chain.batch(b.n)
                dve.wait_ge(x_loaded[b.par], 16 * b.half + 16)
                dve.sem_inc(dve_held, 1)
                for t in range(QT):
                    chain.mark(nc.vector.bn_stats(st6[:, 0, t, :], xs[:, bass.ds(QT * b.n + t, 1), :].rearrange("p a h -> p (a h)")))
                chain.settle()
                dve.sem_inc(dve_held, 1)
                for t in range(QT):
                    chain.mark(nc.vector.bn_aggr(mv[:, 0, t, :], st6[:, 0, t, :]))
                chain.settle()
                nc.vector.tensor_scalar(mv[:, 0, :, 1], mv[:, 0, :, 1], LN_EPS, None, ALU.add).then_inc(x_var, 1)
            elif piece == "xn":
                dve.wait_ge(x_rstd, b.n + 1)
                for t in range(QT):
                    nc.vector.tensor_scalar(xn[:, t, :], xs[:, bass.ds(QT * b.n + t, 1), :].rearrange("p a h -> p (a h)"),
                                            mv[:, 0, t, 0:1], rstd[:, 0, t : t + 1], ALU.subtract, ALU.mult)\
                      .then_inc(xn_ready, 1)
            elif piece == "c":
                dve.wait_ge(c_loaded[b.par], 16 * b.half + 16)
                for t in range(QT):
                    at.dve_lo(dve, b, t, xn[:, t, :], SC_N, chain)
                for t in range(QT):
                    at.dve_lo(dve, b, QT + t, cbuf[:, b.par, t, :], SC_C, chain)
                chain.end("prep0")
            else:
                at.dve_stack(dve, b, piece)

        def pe_post0(pe, b, piece):
            use = ["o0", "o1", "x0", "x1", "g", "pos"]
            if piece not in use:
                return
            k = use.index(piece)
            pe.wait_ge(post_read, M_POST * b.n + k + 1)
            if piece[0] == "o":
                t = int(piece[1])
                pe.wait_ge(at.out_read, 2 * b.n + t + 2)
                for c in range(HC):
                    last = nc.tensor.transpose(mPost[:, c * P : (c + 1) * P], at.outT[:, b.par, t, c * P : (c + 1) * P], id32[:])
            elif piece[0] == "x":
                t = int(piece[1])
                pe.wait_ge(xe_norm, QT * b.n + t + 1)
                for c in range(HC):
                    last = nc.tensor.transpose(mPost[:, c * P : (c + 1) * P], xe[:, b.par, t, c * P : (c + 1) * P], id32[:])
            elif piece == "g":
                for t in range(QT):
                    for c in range(HC):
                        last = nc.tensor.matmul(mPost[:, t * E : (t + 1) * E], xeT[:, t, c * P : (c + 1) * P], gw[:, c, :],
                                                start=c == 0, stop=c == HC - 1)
            else:
                pe.wait_ge(chosen_r, b.n + 1)
                for t in range(QT):
                    nc.tensor.matmul(mPost[:, t * E : (t + 1) * E], tri[:], chosen16[:, t, :], start=True, stop=False)
                    last = nc.tensor.matmul(mPost[:, t * E : (t + 1) * E], ones[:], cum[:, t, :], start=False, stop=True)
            last.then_inc(post_ps, 1)

        def act_post0(act, b, piece):
            if piece == "r1":
                act.wait_ge(gate_shift, b.n + 1)
                nc.scalar.activation(ex[:, :, :], lgm[:, :, :], ACT.Exp).then_inc(gate_exp, 1)

        def pool_post0(pool, b, piece):
            if piece == "o1":
                pool.wait_ge(p_var, b.n + 1)
                nc.gpsimd.tensor_tensor(rstd[:, 1, :], mv[:, 1, :, 1], neghalf[:, 0:QT], ALU.pow).then_inc(p_rstd, 1)

        def pool_send(pool, b, k):
            if k == 0:
                pool.wait_ge(slots_sent[b.prev().par], 16 * QT * TOPK * (b.prev().half + 1) + 16)
                pool.sem_inc(slots_free, 1)
                pool.wait_ge(slots_ready, b.n + 1)
                pool.sem_inc(pool_post, 1)
            nc.gpsimd.indirect_dma_start(slots, bass.IndirectOffsetOnAxis(ap=slot_ix[:, b.par, k // TOPK, k % TOPK : k % TOPK + 1], axis=0),
                                         tok[:, b.par, k // TOPK : k // TOPK + 1], None,
                                         bounds_check=E * CAP - 1, oob_is_err=False).then_inc(slots_sent[b.par], 16)

        K_POST0 = 25

        def dve_post0(dve, b, piece, chain):
            def mine(t):
                return xs[:, bass.ds(QT * b.n + t, 1), :].rearrange("p a h -> p (a h)") if not isinstance(b.n, int) else xs[:, QT * b.n + t, :]

            if piece[0] == "o":
                t = int(piece[1])
                if t == 0:
                    chain.batch(b.n)
                    dve.wait_ge(at.probs_made, STEPS * b.n + STEPS)
                    chain.link(nc.vector.reciprocal(rsum[:, :, :], at.sums[:, b.par, :, :]))
                dve.wait_ge(post_ps, M_POST * b.n + t + 1)
                nc.vector.tensor_tensor(att[:, :].rearrange("p (h d) -> p h d", d=D), mPost[:, :].rearrange("p (h d) -> p h d", d=D),
                                        rep(rsum[:, t, :], D, 2), ALU.mult).then_inc(post_read, 1)
                dve.wait_ge(post_read, M_POST * b.n + t + 2)
                chain.link(nc.vector.scalar_tensor_tensor(mine(t), att[:, :], gates[:, 0:1], mine(t), ALU.mult, ALU.add))
                dve.sem_inc(dve_held, 1)
                chain.link(nc.vector.bn_stats(st6[:, 1, t, :], mine(t)))
                dve.sem_inc(dve_held, 1)
                chain.link(nc.vector.bn_aggr(mv[:, 1, t, :], st6[:, 1, t, :]))
                if t == QT - 1:
                    nc.vector.tensor_scalar(mv[:, 1, :, 1], mv[:, 1, :, 1], LN_EPS, None, ALU.add).then_inc(p_var, 1)
            elif piece == "n":
                dve.wait_ge(p_rstd, b.n + 1)
                dve.wait_ge(xe_free, b.n + 1)
                for t in range(QT):
                    nc.vector.tensor_scalar(xe[:, b.par, t, 0:H], mine(t), mv[:, 1, t, 0:1], rstd[:, 1, t : t + 1],
                                            ALU.subtract, ALU.mult).then_inc(xe_norm, 1)
            elif piece[0] == "x":
                t = int(piece[1])
                dve.wait_ge(post_ps, M_POST * b.n + 3 + t)
                nc.vector.tensor_copy(xeT[:, t, :], mPost[:, :]).then_inc(post_read, 1)
            elif piece == "r1":
                dve.wait_ge(post_ps, M_POST * b.n + 5)
                nc.vector.tensor_copy(lg[:, :, :], mPost[:, 0 : QT * E].rearrange("p (t e) -> p t e", e=E)).then_inc(post_read, 1)
                dve.wait_ge(post_read, M_POST * b.n + 6)
                dve.sem_inc(dve_held, 1)
                for t in range(QT):
                    chain.mark(nc.vector.max(top[:, t, :], lg[:, t, :]))
                chain.settle()
                nc.vector.tensor_tensor(lgm[:, :, :], lg[:, :, :], rep(top[:, :, 0], E, 2), ALU.subtract).then_inc(gate_shift, 1)
                for t in range(QT):
                    chain.mark(nc.vector.match_replace(rp[:, t, :], top[:, t, :], lg[:, t, :], MASKED))
                chain.settle()
                chain.link(nc.vector.tensor_tensor(chosen[:, :, :], lg[:, :, :], rp[:, :, :], ALU.not_equal))
                chain.link(nc.vector.tensor_copy(cum[:, 0, :], cum[:, QT, :]))
                for t in range(QT):
                    chain.link(nc.vector.tensor_tensor(cum[:, t + 1, :], cum[:, t, :], chosen[:, t, :], ALU.add))
                nc.vector.tensor_copy(chosen16[:, :, :], chosen[:, :, :]).then_inc(chosen_r, 1)
            elif piece == "r2":
                dve.wait_ge(gate_exp, b.n + 1)
                chain.link(nc.vector.tensor_tensor(ex[:, :, :], ex[:, :, :], chosen[:, :, :], ALU.mult))
                chain.link(nc.vector.tensor_reduce(ws[:, :], ex[:, :, :], AX, ALU.add))
                chain.link(nc.vector.reciprocal(ws[:, :], ws[:, :]))
                chain.link(nc.vector.tensor_scalar(ws[:, :], ws[:, :], 1.0 / (SC_H * SC_W), None, ALU.mult))
                nc.vector.tensor_tensor(xe[:, b.par, :, H:ROW], ex[:, :, :], rep(ws[:, :], E, 2), ALU.mult).then_inc(xe_full, 1)
                dve.wait_ge(post_ps, M_POST * b.n + 6)
                pos = mPost[:, 0 : QT * E].rearrange("p (t e) -> p t e", e=E)
                chain.mark(nc.vector.tensor_tensor(slot1[:, :, :], pos, rep(eoff[:, :], QT, 1), ALU.add))
                nc.vector.scalar_tensor_tensor(kept[:, :, :], pos, float(CAP), chosen[:, :, :], ALU.is_lt, ALU.mult).then_inc(post_read, 1)
                chain.settle()
                dve.wait_ge(post_read, M_POST * b.n + 7)
                chain.link(nc.vector.tensor_tensor(key[:, :, :], slot1[:, :, :], kept[:, :, :], ALU.mult))
                dve.sem_inc(dve_held, 1)
                for t in range(QT):
                    chain.mark(nc.vector.max(k8[:, t, :], key[:, t, :]))
                chain.settle()
                chain.link(nc.vector.tensor_scalar(far[:, :, :], k8[:, :, :], 0.0, FAR, ALU.is_equal, ALU.mult))
                dve.wait_ge(slots_free, b.n + 1)
                chain.mark(nc.vector.tensor_copy(tok[:, b.par, :], token_ids[:, bass.ds(QT * b.n, QT)]))
                nc.vector.scalar_tensor_tensor(slot_ix[:, b.par, :, :], k8[:, :, :], -1.0, far[:, :, :], ALU.add, ALU.add)\
                  .then_inc(slots_ready, 1)
                chain.end("post0")

        def slot_pieces(table, s):
            return table.get(s, [])

        @block.sync
        def _(sp):
            sp.dma_start(gates_in[:, 0:2], broadcast_rows(g_xattn, P)).then_inc(c_in, 16)
            sp.dma_start(gates_in[:, 2:4], broadcast_rows(g_ffn, P)).then_inc(c_in, 16)
            sp.dma_start(gw[:, :, :], gate_w.rearrange("(c p) e -> p c e", p=P)).then_inc(c_in, 16)

            xv = x.rearrange("b (t p) h -> b p t h", p=P)
            cv = ctx.rearrange("b (t p) h -> b p t h", p=P)

            def load(b):
                bi = b.n if isinstance(b.n, int) else bass.ds(b.n, 1)
                src = (lambda v: v[b.n]) if isinstance(b.n, int) else (lambda v: v[bass.ds(b.n, 1)].rearrange("a p t h -> p (a t) h"))
                sp.dma_start(xs[:, bass.ds(QT * b.n, QT), :], src(xv)).then_inc(x_loaded[b.par], 16)
                sp.dma_start(cbuf[:, b.par, :, :], src(cv)).then_inc(c_loaded[b.par], 16)

            def store(b):
                sp.wait_ge(xe_full, b.n + 1)
                dst = tokens[bass.ds(QT * P * b.n, QT * P), :].rearrange("(t p) h -> p t h", p=P)
                sp.dma_start(dst, xe[:, b.par, :, :]).then_inc(xe_stored[b.par], 16)
                sp.wait_ge(xe_stored[b.par], 16 * b.half + 16)
                sp.sem_inc(xe_free, 1)

            def body(b):
                sp.wait_ge(at.out_made, 2 * b.prev().n + 2)
                load(b.next())
                store(b.prev())

            sp.sem_inc(xe_free, 2)
            load(Batch(0, 0, 0))
            load(Batch(1, 1, 0))
            sp.wait_ge(consts, N_CONST)
            sp.dma_start(tokens[T : T + P, :], zeros[:, :]).then_inc(zero_in, 16)
            for i in range(2):
                sp.dma_start(acc[i].rearrange("(t p) h -> p t h", p=P), rep(zeros[:, 0:H], T // P + 1, 1)).then_inc(zero_in, 16)
            over_batches(sp, lambda b: None, body, lambda b: store(b.prev()))
            store(Batch(B - 1, 1, (B - 1) // 2))
            sp.wait_ge(zero_in, 48)

        @block.gpsimd
        def _(pool):
            g = nc.gpsimd
            n = [0]

            def const(ins):
                ins.then_inc(consts, 1)
                n[0] += 1
                pool.wait_ge(consts, n[0])

            def select(m, op, fill, base, step, mult):
                const(g.affine_select(out=m, in_=m, compare_op=op, fill=fill, base=base, pattern=[[step, m.shape[-1]]],
                                      channel_multiplier=mult))

            for m in (id32, id16, idb):
                const(g.memset(m[:], 0.0))
                select(m[:], ALU.not_equal, 1.0, 0, -1, 1)
            const(g.memset(maskb[:], 0.0))
            select(maskb[:], ALU.is_ge, MASKED, 0, -1, 1)
            const(g.memset(tri[:], 1.0))
            select(tri[:], ALU.is_gt, 0.0, 0, 1, -1)
            const(g.memset(shift[:], 0.0))
            for i, by in enumerate((1, NW)):
                select(shift[:, i, :], ALU.not_equal, 1.0, by, -1, 1)
            const(g.memset(ones[:], 1.0))
            const(g.memset(shared.ones32[:], 1.0))
            const(g.memset(neghalf[:], -0.5))
            const(g.memset(zeros[:], 0.0))
            io = dict(allow_small_or_imprecise_dtypes=True)
            const(g.iota(eoff[:], pattern=[[CAP, E]], base=1, channel_multiplier=0, **io))
            const(g.iota(token_ids[:], pattern=[[P, T // P + 1]], base=0, channel_multiplier=1, **io))
            const(g.iota(pads[:], pattern=[[1, P]], base=T, channel_multiplier=0, **io))
            const(g.iota(thr[:], pattern=[[P, TPE - 1]], base=P, channel_multiplier=0, **io))
            const(g.iota(tiles_iota[:], pattern=[[1, MT]], base=0, channel_multiplier=0, **io))
            assert n[0] == N_CONST, n[0]
            pool.sem_inc(slots_free, 1)
            for i in range(2):
                pool.dma_start(slots[i * E * CAP // 2 : (i + 1) * E * CAP // 2, :].rearrange("(p c) a -> p (c a)", p=P), pads[:, :])\
                  .then_inc(slots_sent[i], 16)
            for i in range(2):
                pool.wait_ge(slots_sent[i], 16)

            b0 = Batch(0, 0, 0)
            for pieces in PREP0.values():
                for piece in pieces:
                    pool_prep0(pool, b0, piece)

            def body(b, prep, post):
                sent = 0
                for s in range(STEPS):
                    for piece in slot_pieces(POST0, s) if post else []:
                        pool_post0(pool, b.prev(), piece)
                    for k in range(SENDS.get(s, 0) if post else 0):
                        pool_send(pool, b.prev(), sent)
                        sent += 1
                    for piece in slot_pieces(PREP0, s) if prep else []:
                        pool_prep0(pool, b.next(), piece)

            over_batches(pool, lambda b: body(b, True, False), lambda b: body(b, True, True), lambda b: body(b, False, True))
            end = Batch(B - 1, 1, (B - 1) // 2)
            for piece in sum(POST0.values(), []):
                pool_post0(pool, end, piece)
            for k in range(QT * TOPK):
                pool_send(pool, end, k)
            for i in range(2):
                pool.wait_ge(slots_sent[i], 16 * QT * TOPK * B // 2 + 16)

        @block.scalar
        def _(act):
            nc.scalar.preload_act_table(ACT.Exp)
            act.wait_ge(c_in, 48)
            nc.scalar.activation(gates[:, :], gates_in[:, :], ACT.Tanh).then_inc(gates_ready, 1)
            b0 = Batch(0, 0, 0)
            for pieces in PREP0.values():
                for piece in pieces:
                    act_prep0(act, b0, piece)
            at.act_exp(act, b0, 0)

            def body(b, prep, post, more):
                for s in range(STEPS):
                    at.act_step(act, b, s, more)
                    for piece in slot_pieces(POST0, s) if post else []:
                        act_post0(act, b.prev(), piece)
                    for piece in slot_pieces(PREP0, s) if prep else []:
                        act_prep0(act, b.next(), piece)

            over_batches(act, lambda b: body(b, True, False, True), lambda b: body(b, True, True, True),
                         lambda b: body(b, False, True, False))
            for piece in sum(POST0.values(), []):
                act_post0(act, Batch(B - 1, 1, (B - 1) // 2), piece)

        @block.vector
        def _(dve):
            prep, post = Chain(dve, dve_prep, K_PREP0), Chain(dve, dve_post, K_POST0)
            nc.vector.memset(cum[:], 0.0).then_inc(start_dve, 1)
            dve.wait_ge(start_dve, 1)
            dve.sem_inc(at.stack_ready, 1)
            dve.sem_inc(post_read, 1)
            dve.sem_inc(at.out_read, 1)
            dve.wait_ge(consts, N_CONST)
            dve.wait_ge(gates_ready, 1)
            b0 = Batch(0, 0, 0)
            for pieces in PREP0.values():
                for piece in pieces:
                    dve_prep0(dve, b0, piece, prep)
            at.dve_max(dve, b0, 0)
            at.dve_max(dve, b0, 1)

            def body(b, do_prep, do_post, more):
                for s in range(STEPS):
                    at.dve_step(dve, b, s, more, before=do_post)
                    for piece in slot_pieces(POST0, s) if do_post else []:
                        dve_post0(dve, b.prev(), piece, post)
                    for piece in slot_pieces(PREP0, s) if do_prep else []:
                        dve_prep0(dve, b.next(), piece, prep)

            over_batches(dve, lambda b: body(b, True, False, True), lambda b: body(b, True, True, True),
                         lambda b: body(b, False, True, False))
            end = Batch(B - 1, 1, (B - 1) // 2)
            at.dve_out(dve, end, 1)
            for piece in sum(POST0.values(), []):
                dve_post0(dve, end, piece, post)

        @block.tensor
        def _(pe):
            pe.sem_inc(at.stack_ps, 8)
            pe.wait_ge(consts, N_CONST)
            pe.wait_ge(c_in, 48)
            b0 = Batch(0, 0, 0)
            for pieces in PREP0.values():
                for piece in pieces:
                    pe_prep0(pe, b0, piece)
            pe.wait_ge(at.stack_ready, 9)
            at.pe_scores(b0, 0)
            at.pe_scores(b0, 1)

            def body(b, prep, post, more):
                for s in range(STEPS):
                    at.pe_step(pe, b, s, more, before=post)
                    for piece in slot_pieces(POST0, s) if post else []:
                        pe_post0(pe, b.prev(), piece)
                    for piece in slot_pieces(PREP0, s) if prep else []:
                        pe_prep0(pe, b.next(), piece)

            over_batches(pe, lambda b: body(b, True, False, True), lambda b: body(b, True, True, True),
                         lambda b: body(b, False, True, False))
            end = Batch(B - 1, 1, (B - 1) // 2)
            at.pe_pv(pe, end, STEPS - 1)
            for piece in sum(POST0.values(), []):
                pe_post0(pe, end, piece)


class Tile:

    def __init__(self, n, place, oct):
        self.n, self.place, self.oct = n, place, oct

    def at(self, d):
        q, place = divmod(self.place + d, 8)
        return Tile(self.n + d, place, self.oct + q)

    def exists(self):
        return not isinstance(self.n, int) or 0 <= self.n < MT

    def column(self):
        return slice(self.n, self.n + 1) if isinstance(self.n, int) else bass.ds(self.n, 1)


def over_tiles(eng, step):
    first, last = 5, 3
    for t in range(first):
        step(Tile(t, t, 0))
    with eng.Fori(0, (MT - first - last) // 8) as i:
        for k in range(8):
            q, place = divmod(first + k, 8)
            step(Tile(8 * i + first + k, place, i + q))
    for t in range(MT - last, MT):
        step(Tile(t, t % 8, t // 8))


def experts(nc, shared, w_experts):
    es = ExitStack()
    with es:

        def sb(name, shape, dt=F32):
            return es.enter_context(nc.sbuf_tensor(name, shape, dt))

        def sem(name):
            return es.enter_context(nc.semaphore(name))

        def sems(name, n):
            return [sem(f"{name}{i}") for i in range(n)]

        bank = shared.bank
        bX, bGU, bHT, bY = bank[0:2], bank[2:4], bank[4:6], bank[6:8]

        slot_rows = sb("slot_rows", [P, 2, P])
        idx_all = sb("idx_all", [P, 2 * P + 1], I32)
        counts = sb("counts", [E, 1])
        over = sb("over", [E, TPE - 1])
        tiles = sb("tiles", [E, 1])
        tiles16 = sb("tiles16", [E, 1], F16)
        first_t = sb("first_t", [E, 1])
        before16 = sb("before16", [E, 2], F16)
        begun = sb("begun", [E, MT], F16)
        row_e1, row_f, row_w, row_a, row_b = (sb(f"row{i}", [1, MT]) for i in range(5))
        t_e1 = sb("t_e1", [1, MT], I32)
        t_slot = sb("t_slot", [1, MT], I32)
        t_freed = sb("t_freed", [1, MT], I32)
        t_col = sb("t_col", [1, MT], I32)
        t_new = sb("t_new", [1, MT + 8], I32)

        ix = sb("ix", [P, 8], I32)
        xg = sb("xg", [P, 8, ROW])
        xh = sb("xh", [P, 2, H], F16)
        xl = sb("xl", [P, 2, H], F16)
        sg = sb("sg", [P, 2, FI])
        hv = sb("hv", [P, FI])
        hp = sb("hp", [P, 2, 2 * FI], F16)
        hT = sb("hT", [P, 2, 3 * P], F16)
        ysb = sb("ysb", [P, NY, H])
        raw = sb("raw", [P, NW, WEXP])
        wh = sb("wh", [P, NW, WEXP], F16)
        wl = sb("wl", [P, NW, WEXP], F16)

        rows_in = sem("rows_in")
        tab_ps, tab = sem("tab_ps"), sem("tab")
        w_in, raw_ready, w_hi, weights_ready = sems("w_in", NW), sem("raw_ready"), sem("w_hi"), sem("weights_ready")
        ix_ready, gathered, added, y_free = sem("ix_ready"), sems("gathered", 8), sems("added", NY), sem("y_free")
        pool_held = sem("pool_held")
        x_ps, x_hi, x_ready = sem("x_ps"), sem("x_hi"), sem("x_ready")
        gu_ps, silu, h_made, h_hi, h_ready = sem("gu_ps"), sem("silu"), sem("h_made"), sem("h_hi"), sem("h_ready")
        ht_ps, ht_ready, y_ps, y_ready = sem("ht_ps"), sem("ht_ready"), sem("y_ps"), sem("y_ready")
        TAB_PE, TAB_DVE = 4, 24

        block = es.enter_context(nc.Block())

        @block.sync
        def _(sp):
            sp.dma_start(slot_rows[:, :, :], shared.slots.rearrange("(a p c) o -> p a (c o)", a=2, c=P)).then_inc(rows_in, 16)

            def load(e, slot, e3, wait, before):
                if wait:
                    sp.wait_ge(weights_ready, e - NW + 1)
                src = w_experts[e] if isinstance(e, int) else w_experts[bass.ds(e, 1)].rearrange("a p w -> p (a w)")
                sp.dma_start(raw[:, slot, :], src).then_inc(w_in[slot], 16)
                if before:
                    sp.wait_ge(w_in[(slot - 1) % NW], 16 * (e3 + (0 if slot == 0 else 1)))
                    sp.sem_inc(raw_ready, 1)

            for e in range(NW):
                load(e, e, 0, False, e > 0)
            with sp.Fori(0, (E - NW) // NW) as i:
                for k in range(NW):
                    load(NW * i + NW + k, k, i + 1, True, True)
            for e in range(E // NW * NW, E):
                load(e, e % NW, e // NW, True, True)
            sp.wait_ge(w_in[(E - 1) % NW], 16 * ((E - 1) // NW + 1))
            sp.sem_inc(raw_ready, 1)

        @block.gpsimd
        def _(pool):
            def gather(t):
                col = pool.value_load(t_col[0:1, t.column()], min_val=0, max_val=2 * P)
                nc.gpsimd.tensor_copy(ix[:, t.place : t.place + 1], idx_all[:, bass.ds(col, 1)]).then_inc(ix_ready, 1)
                pool.wait_ge(ix_ready, t.n + 1)
                pool.sem_inc(pool_held, 1)
                nc.gpsimd.indirect_dma_start(xg[:, t.place, :], None, shared.tokens,
                                             bass.IndirectOffsetOnAxis(ap=ix[:, t.place : t.place + 1], axis=0))\
                  .then_inc(gathered[t.place], 16)

            def add(t):
                pool.wait_ge(y_ready, t.n + 1)
                b = t.at(-2)
                if b.exists():
                    pool.wait_ge(added[b.place % NY], 16 * (2 * b.oct + b.place // NY + 1))
                pool.sem_inc(y_free, 1)
                nc.gpsimd.indirect_dma_start(shared.acc[t.place % 2],
                                             bass.IndirectOffsetOnAxis(ap=ix[:, t.place : t.place + 1], axis=0),
                                             ysb[:, t.place % NY, :], None, compute_op=ALU.add)\
                  .then_inc(added[t.place % NY], 16)

            pool.wait_ge(tab, TAB_DVE)
            for t in range(3):
                gather(Tile(t, t, 0))

            def step(t):
                if t.at(-3).exists():
                    add(t.at(-3))
                if t.at(3).exists():
                    gather(t.at(3))

            over_tiles(pool, step)
            for t in range(MT - 3, MT):
                add(Tile(t, t % 8, t // 8))
            for i in range(NY):
                pool.wait_ge(added[i], 16 * (MT // NY))

        @block.tensor
        def _(pe):
            id32, id16 = shared.id32, shared.id16
            pe.wait_ge(rows_in, 16)
            for a in range(2):
                nc.tensor.transpose(bX[0][:, a * P : (a + 1) * P], slot_rows[:, a, :], id32[:])
            nc.tensor.matmul(bX[0][0:E, 2 * P : 2 * P + 1], shared.cum[:, QT, :], shared.ones[:, 0:1], start=True, stop=True)\
              .then_inc(tab_ps, 1)
            pe.wait_ge(tab, 6)
            nc.tensor.matmul(bX[1][0:E, 0:1], shared.tri[0:E, 0:E], tiles16[:, :], start=True, stop=True)
            nc.tensor.matmul(bX[1][0:E, 1:2], shared.shift[:, 0, :], tiles16[:, :], start=True, stop=True)
            nc.tensor.matmul(bX[1][0:E, 2:3], shared.shift[:, 1, :], tiles16[:, :], start=True, stop=True).then_inc(tab_ps, 1)
            pe.wait_ge(tab, 9)
            nc.tensor.matmul(bGU[0][0:1, 0:MT], shared.ones[0:E, 0:1], begun[:, :], start=True, stop=True)
            nc.tensor.matmul(bGU[1][0:1, 0:MT], before16[:, 0:1], begun[:, :], start=True, stop=True)
            nc.tensor.matmul(bHT[0][0:1, 0:MT], before16[:, 1:2], begun[:, :], start=True, stop=True).then_inc(tab_ps, 1)
            pe.sem_inc(y_ps, 1)

            def turn(t):
                pe.wait_ge(gathered[t.place], 16 * t.oct + 16)
                if t.at(-2).exists():
                    pe.wait_ge(x_ready, t.n - 1)
                for c in range(HC):
                    last = nc.tensor.transpose(bX[t.place % 2][:, c * P : (c + 1) * P], xg[:, t.place, c * P : (c + 1) * P], id32[:])
                last.then_inc(x_ps, 1)

            def gate_up(t):
                e1 = pe.value_load(t_e1[0:1, t.column()], min_val=1, max_val=E)
                w = pe.value_load(t_slot[0:1, t.column()], min_val=0, max_val=NW - 1)
                pe.wait_ge(x_ready, t.n + 1)
                pe.wait_ge(weights_ready, e1)
                if t.at(-2).exists():
                    pe.wait_ge(h_ready, t.n - 1)
                passes = [(xh, wh), (xh, wl), (xl, wh)]
                for c in range(HC):
                    for k, (xp, wp) in enumerate(passes):
                        last = nc.tensor.matmul(bGU[t.place % 2][:, 0:GU], xp[:, t.place % 2, c * P : (c + 1) * P],
                                                wp[:, bass.ds(w, 1), c * GU : (c + 1) * GU].rearrange("p a w -> p (a w)"),
                                                start=c == 0 and k == 0, stop=c == HC - 1 and k == 2)
                last.then_inc(gu_ps, 1)

            def turn_h(t):
                pe.wait_ge(h_ready, t.n + 1)
                if t.at(-2).exists():
                    pe.wait_ge(ht_ready, t.n - 1)
                o = bHT[t.place % 2][:, :].bitcast(F16)
                for c in range(3):
                    last = nc.tensor.transpose(o[:, c * P : (c + 1) * P], hp[:, t.place % 2, c * P : (c + 1) * P], id16[:])
                last.then_inc(ht_ps, 1)

            def down(t):
                w = pe.value_load(t_slot[0:1, t.column()], min_val=0, max_val=NW - 1)
                pe.wait_ge(ht_ready, t.n + 1)
                if t.at(-2).exists():
                    pe.wait_ge(y_ready, t.n - 1)
                hi, lo, rest = (hT[:, t.place % 2, c * P : (c + 1) * P] for c in range(3))
                full, part = HC * GU, HC * GU + H
                products = [(hi, wh, full, P), (hi, wl, full, P), (lo, wh, full, P), (rest, wh, part, P),
                            (rest, wl, part, FI - P)]
                for k, (h, wp, at, rows) in enumerate(products):
                    last = nc.tensor.matmul(bY[t.place % 2][:, :], h[0:rows, :],
                                            wp[0:rows, bass.ds(w, 1), at : at + H].rearrange("p a w -> p (a w)"),
                                            start=k == 0, stop=k == len(products) - 1)
                last.then_inc(y_ps, 1)

            def step(t):
                if t.at(1).exists():
                    turn(t.at(1))
                gate_up(t)
                if t.at(-1).exists():
                    turn_h(t.at(-1))
                if t.at(-2).exists():
                    down(t.at(-2))

            pe.wait_ge(tab, TAB_DVE)
            turn(Tile(0, 0, 0))
            over_tiles(pe, step)
            last = Tile(MT - 1, (MT - 1) % 8, (MT - 1) // 8)
            turn_h(last)
            down(last.at(-1))
            down(last)

        @block.scalar
        def _(act):
            def hi(t):
                act.wait_ge(x_ps, t.n + 1)
                if t.at(-2).exists():
                    act.wait_ge(gu_ps, t.n - 1)
                nc.scalar.activation(xh[:, t.place % 2, :], bX[t.place % 2][:, :], ACT.Copy, scale=SC_N).then_inc(x_hi, 1)

            def silu_of(t):
                act.wait_ge(gu_ps, t.n + 1)
                if t.at(-2).exists():
                    act.wait_ge(h_made, t.n - 1)
                nc.scalar.activation(sg[:, t.place % 2, :], bGU[t.place % 2][:, 0:FI], ACT.Silu, scale=1.0 / (SC_N * SC_W))\
                  .then_inc(silu, 1)

            def copy_h(t):
                act.wait_ge(ht_ps, t.n + 1)
                if t.at(-2).exists():
                    act.wait_ge(y_ps, t.n)
                nc.scalar.activation(hT[:, t.place % 2, :], bHT[t.place % 2][:, :].bitcast(F16)[:, 0 : 3 * P], ACT.Copy)\
                  .then_inc(ht_ready, 1)

            def weigh(t):
                e1 = act.value_load(t_e1[0:1, t.column()], min_val=1, max_val=E)
                act.wait_ge(y_ps, t.n + 2)
                if t.at(-NY).exists():
                    act.wait_ge(y_free, t.n - 1)
                nc.scalar.activation(ysb[:, t.place % NY, :], bY[t.place % 2][:, :], ACT.Copy,
                                     scale=xg[:, t.place, bass.ds(e1 + (H - 1), 1)]).then_inc(y_ready, 1)

            nc.scalar.preload_act_table(ACT.Silu)
            act.wait_ge(tab, TAB_DVE)
            hi(Tile(0, 0, 0))

            def step(t):
                if t.at(1).exists():
                    hi(t.at(1))
                silu_of(t)
                if t.at(-1).exists():
                    copy_h(t.at(-1))
                if t.at(-2).exists():
                    weigh(t.at(-2))

            over_tiles(act, step)
            last = Tile(MT - 1, (MT - 1) % 8, (MT - 1) // 8)
            copy_h(last)
            weigh(last.at(-1))
            weigh(last)

        @block.vector
        def _(dve):
            v, chain = nc.vector, Chain(dve, tab, 0)
            dve.wait_ge(tab_ps, 1)
            chain.mark(v.tensor_copy(idx_all[:, 0 : 2 * P], bX[0][:, 0 : 2 * P]))
            chain.mark(v.tensor_copy(idx_all[:, 2 * P : 2 * P + 1], shared.token_ids[:, T // P : T // P + 1]))
            chain.link(v.tensor_copy(counts[:, :], bX[0][0:E, 2 * P : 2 * P + 1]))
            chain.link(v.tensor_scalar(over[:, :], shared.thr[:, :], counts[:, 0:1], None, ALU.is_lt))
            chain.link(v.tensor_reduce(tiles[:, :], over[:, :], AX, ALU.add))
            chain.mark(v.tensor_scalar(tiles16[:, :], tiles[:, :], 1.0, None, ALU.add))
            assert chain.n == 6
            dve.wait_ge(tab_ps, 2)
            chain.link(v.tensor_copy(first_t[:, :], bX[1][0:E, 0:1]))
            chain.mark(v.tensor_copy(before16[:, :], bX[1][0:E, 1:3]))
            chain.mark(v.tensor_scalar(begun[:, :], shared.tiles_iota[:, :], first_t[:, 0:1], None, ALU.is_ge))
            assert chain.n == 9
            dve.wait_ge(tab_ps, 3)
            chain.mark(v.tensor_copy(row_e1[:, :], bGU[0][0:1, 0:MT]))
            chain.mark(v.tensor_copy(row_w[:, :], bHT[0][0:1, 0:MT]))
            chain.link(v.tensor_copy(row_f[:, :], bGU[1][0:1, 0:MT]))
            chain.mark(v.tensor_copy(t_e1[:, :], row_e1[:, :]))
            chain.mark(v.tensor_copy(t_freed[:, :], row_w[:, :]))
            chain.link(v.scalar_tensor_tensor(row_a[:, :], row_e1[:, :], float(TPE), row_f[:, :], ALU.mult, ALU.subtract))
            chain.link(v.tensor_tensor(row_a[:, :], row_a[:, :], shared.tiles_iota[0:1, :], ALU.add))
            chain.link(v.tensor_scalar(t_col[:, :], row_a[:, :], float(-TPE), float(2 * P), ALU.add, ALU.min))
            chain.link(v.tensor_scalar(row_a[:, :], row_e1[:, :], 1.0 / NW, -2.0 / NW, ALU.mult, ALU.add))
            chain.link(v.tensor_scalar(row_a[:, :], row_a[:, :], ROUND, -ROUND, ALU.add, ALU.add))
            chain.link(v.scalar_tensor_tensor(row_b[:, :], row_a[:, :], float(-NW), row_e1[:, :], ALU.mult, ALU.add))
            chain.mark(v.tensor_scalar(t_slot[:, :], row_b[:, :], -1.0, None, ALU.add))
            chain.mark(v.memset(t_new[:, :], 0))
            chain.settle()
            chain.link(v.tensor_tensor(row_a[:, 1:MT], row_e1[:, 1:MT], row_e1[:, 0 : MT - 1], ALU.subtract))
            chain.link(v.tensor_copy(t_new[:, 1:MT], row_a[:, 1:MT]))
            assert chain.n == TAB_DVE, chain.n

            def lo(t):
                dve.wait_ge(x_hi, t.n + 1)
                v.scalar_tensor_tensor(xl[:, t.place % 2, :], bX[t.place % 2][:, :], SC_N, xh[:, t.place % 2, :],
                                       ALU.mult, ALU.subtract).then_inc(x_ready, 1)

            def hidden(t):
                dve.wait_ge(silu, t.n + 1)
                if t.exists() and t.at(-1).exists():
                    dve.wait_ge(h_ready, t.n)
                v.scalar_tensor_tensor(hv[:, :], bGU[t.place % 2][:, FI:GU], SC_H / (SC_N * SC_W), sg[:, t.place % 2, :],
                                       ALU.mult, ALU.mult).then_inc(h_made, 1)
                dve.wait_ge(h_made, t.n + 1)
                if t.at(-2).exists():
                    dve.wait_ge(ht_ps, t.n - 1)
                p, rest = hp[:, t.place % 2, :], FI - P
                v.tensor_copy(p[:, 0:P], hv[:, 0:P]).then_inc(h_hi, 1)
                v.tensor_copy(p[:, 2 * P : 2 * P + rest], hv[:, P:FI]).then_inc(h_hi, 1)
                dve.wait_ge(h_hi, 2 * t.n + 2)
                v.tensor_tensor(p[:, P : 2 * P], hv[:, 0:P], p[:, 0:P], ALU.subtract)
                v.tensor_tensor(p[:, 2 * P + rest :], hv[:, P:FI], p[:, 2 * P : 2 * P + rest], ALU.subtract).then_inc(h_ready, 1)

            def split(t, free):
                e1 = dve.value_load(t_e1[0:1, t.column()], min_val=1, max_val=E)
                w = dve.value_load(t_slot[0:1, t.column()], min_val=0, max_val=NW - 1)
                if free:
                    f = dve.value_load(t_freed[0:1, t.column()], min_val=0, max_val=MT - 1)
                    dve.wait_ge(y_ps, f + 1)
                dve.wait_ge(raw_ready, e1)
                pick = lambda m: m[:, bass.ds(w, 1), :].rearrange("p a w -> p (a w)")
                v.tensor_scalar(pick(wh), pick(raw), SC_W, None, ALU.mult).then_inc(w_hi, 1)
                dve.wait_ge(w_hi, e1)
                v.scalar_tensor_tensor(pick(wl), pick(raw), SC_W, pick(wh), ALU.mult, ALU.subtract).then_inc(weights_ready, 1)

            def split_if_new(t, free):
                new = dve.value_load(t_new[0:1, t.column()], min_val=0, max_val=1)
                with dve.If(new > 0):
                    split(t, free)

            chain.settle()
            split(Tile(0, 0, 0), False)
            split_if_new(Tile(1, 1, 0), False)
            lo(Tile(0, 0, 0))

            def step(t):
                if t.at(1).exists():
                    lo(t.at(1))
                hidden(t)
                if t.at(2).exists():
                    split_if_new(t.at(2), True)

            over_tiles(dve, step)


def layer1(nc, shared, ctx, mats, vecs, ternary, out):
    es = ExitStack()
    with es:

        def sb(name, shape, dt=F32):
            return es.enter_context(nc.sbuf_tensor(name, shape, dt))

        def sem(name):
            return es.enter_context(nc.semaphore(name))

        xs, gates, bank = shared.xs, shared.gates, shared.bank
        bSide, bPost, bProj = bank[5], bank[6], bank[7]
        vbuf = sb("vbuf", [P, 2, QT, H])
        at = Attention(nc, sb, sem, bank, "l1_", False, D**-0.5 / (SC_Q * SC_K), vbuf, shared.id32, shared.id16, None, None)

        NM = 5
        w_hi = sb("w_hi", [P, NM, HC * H], F16)
        w_lo = sb("w_lo", [P, NM, HC * H], F16)
        raw = at.stack[:, :, :, :, :].rearrange("p a b h s -> p (a b h s)").bitcast(F32).rearrange("p (m w) -> p m w", m=4)
        raw_t = at.outT[:, :, :, :].rearrange("p a t h -> p (a t h)")
        vec = sb("vec", [P, 7, H])
        B_O, B_T, G_Q, G_K = 3, 4, 5, 6
        absum = sb("absum", [P, HC])
        mean = sb("mean", [P, 2])
        inv = sb("inv", [P, 1])
        sc4 = sb("sc4", [P, 4])

        accb = sb("accb", [P, 2, QT, H])
        proj = accb[:, :, :, :].rearrange("p a t h -> p (a t) h")
        xn = accb[:, 0, :, :]
        cbuf = sb("cbuf1", [P, QT, H])
        halves = at.parts[:, 0:QT, :, :, :].rearrange("p j h a d -> p (j h a d)").rearrange("p (j a h) -> p j a h", j=4, a=2)
        halfT = sb("halfT", [P, 4, 2 * H], F16)
        junk = sb("junk", [P, H])
        ss = sb("ss", [P, 4])
        rs = sb("rs", [P, 4])
        mv = sb("mv1", [P, 2, QT, 2])
        st6 = sb("st61", [P, 2, QT, 6])
        rstd = sb("rstd1", [P, 2, QT])
        rsum = sb("rsum1", [P, QT, NH])
        att = sb("att1", [P, QT, H])
        a16 = sb("a16", [P, QT, 2, H], F16)
        aT = sb("aT", [P, QT, 2 * H], F16)
        outb = sb("outb", [P, QT, H])

        mats_in, vecs_in, tern_in = sem("mats_in"), sem("vecs_in"), sem("tern_in")
        mat_hi, mat_lo, g_made, sc_made = sem("mat_hi"), sem("mat_lo"), sem("g_made"), sem("sc_made")
        abs_made, abs_ps, tern = sem("abs_made"), sem("abs_ps"), sem("tern")
        acc_in, ctx_in = sem("acc_in"), sem("ctx_in")
        x_var, x_rstd, xn_ready = sem("x_var1"), sem("x_rstd1"), sem("xn_ready1")
        half_hi, half_ready = sem("half_hi"), sem("half_ready")
        t_ps, t_read, pj_ps, pj_read = sem("t_ps"), sem("t_read"), sem("pj_ps"), sem("pj_read")
        sq_made, rms_step, rms_ready, q_ready = sem("sq_made"), sem("rms_step"), sem("rms_ready"), sem("q_ready")
        po_ps, po_read, po_copied = sem("po_ps"), sem("po_read"), sem("po_copied")
        a_ready, a_hi, a_lo = sem("a_ready"), sem("a_hi"), sem("a_lo")
        p_var, p_rstd = sem("p_var1"), sem("p_rstd1")
        out_ready, out_free, out_stored = sem("out_ready"), sem("out_free"), sem("out_stored")
        dve_prep, dve_post, dve_held = sem("dve_prep1"), sem("dve_post1"), sem("dve_held1")
        pool_held = sem("pool_held1")

        block = es.enter_context(nc.Block())

        PREP = {0: ["x2"], 1: ["xn"], 2: ["sq"], 3: ["sc"], 4: ["T0", "T1"], 5: ["P0", "T2"], 6: ["P1", "T3"], 7: ["P2"],
                8: ["P3"], 9: ["P4", "r"], 10: ["P5", "h0", "h1"], 11: ["h2", "h3", "S0", "S1"], 12: ["S2", "S3", "S4", "S5"],
                13: ["S6", "S7", "v"]}
        POST = {1: ["a0"], 2: ["a1", "b0"], 3: ["b1", "c0"], 4: ["c1"], 5: ["d0"], 6: ["d1"], 7: ["e"], 8: ["f0", "f1"],
                9: ["g0", "g1"], 10: ["h0"], 11: ["h1"]}
        USES = ["a0", "a1", "c0", "c1", "d0", "d1", "g0", "g1", "h0", "h1"]
        COPIED = ["c0", "c1", "g0", "g1"]
        READ = [u for u in USES if u not in COPIED]

        def pieces(table, s):
            return table.get(s, [])

        def all_pieces(table):
            return [piece for s in sorted(table) for piece in table[s]]

        def mine(b, t):
            if isinstance(b.n, int):
                return xs[:, QT * b.n + t, :]
            return xs[:, bass.ds(QT * b.n + t, 1), :].rearrange("p a h -> p (a h)")

        def products(o, xT, m):
            n = 0
            for c in range(HC):
                for xo, w in ((0, w_hi), (0, w_lo), (H, w_hi)):
                    last = nc.tensor.matmul(o, xT[:, xo + c * P : xo + (c + 1) * P], w[:, m, c * H : (c + 1) * H],
                                            start=n == 0, stop=n == 3 * HC - 1)
                    n += 1
            return last

        def turn16(o, src):
            for k in range(2 * HC):
                last = nc.tensor.transpose(o[:, :].bitcast(F16)[:, k * P : (k + 1) * P], src[:, k // HC, (k % HC) * P : (k % HC + 1) * P],
                                           shared.id16[:])
            return last

        def pe_prep(pe, b, piece):
            k = int(piece[1]) if piece[1:].isdigit() else 0
            if piece[0] == "T":
                pe.wait_ge(half_ready, 4 * b.n + k + 1)
                if k == 0:
                    pe.wait_ge(at.stack_ready, 8 * b.n + 1)
                else:
                    pe.wait_ge(t_read, 4 * b.n + k)
                turn16(bSide, halves[:, k, :, :]).then_inc(t_ps, 1)
            elif piece[0] == "P":
                j = [0, 1, 2, 3, 2, 3][k]
                pe.wait_ge(t_read, 4 * b.n + j + 1)
                if not (isinstance(b.n, int) and 6 * b.n + k == 0):
                    pe.wait_ge(pj_read, 6 * b.n + k)
                products(bProj[:, :], halfT[:, j, :], k // 2).then_inc(pj_ps, 1)
            elif piece[0] == "S":
                if k == 0:
                    pe.wait_ge(t_read, 4 * b.n + 4)
                at.pe_stack(pe, b, k)
            elif piece == "v":
                pe.wait_ge(pj_read, 6 * b.n + 6)

        def source(k):
            return xn[:, k, :] if k < QT else cbuf[:, k - QT, :]

        def act_prep(act, b, piece):
            k = int(piece[1]) if piece[1:].isdigit() else 0
            if piece == "sq":
                act.wait_ge(at.stack_ps, 8 * b.n + 8)
                act.wait_ge(xn_ready, b.n + 1)
                for t in range(QT):
                    nc.scalar.activation(halves[:, t, 0, :], source(t), ACT.Copy, scale=SC_N).then_inc(half_hi, 1)
            elif piece == "sc":
                act.wait_ge(ctx_in, 16 * b.n + 16)
                for t in range(QT):
                    nc.scalar.activation(halves[:, QT + t, 0, :], source(QT + t), ACT.Copy, scale=SC_C).then_inc(half_hi, 1)
            elif piece[0] == "T":
                act.wait_ge(t_ps, 4 * b.n + k + 1)
                if k == 0 and not (isinstance(b.n, int) and b.n == 0):
                    act.wait_ge(pj_ps, 6 * b.n)
                nc.scalar.activation(halfT[:, k, :], bSide[:, :].bitcast(F16), ACT.Copy).then_inc(t_read, 1)
            elif piece[0] == "P" and k < 4:
                act.wait_ge(pj_read, 6 * b.n + k + 1)
                if not (isinstance(b.n, int) and 4 * b.n + k == 0):
                    act.wait_ge(sq_made, 4 * b.n + k)
                nc.scalar.activation(junk[:, :], proj[:, k, :], ACT.Square, accum_out=ss[:, k : k + 1]).then_inc(sq_made, 1)
            elif piece[0] == "h":
                act.wait_ge(q_ready, 2 * b.n + 2)
                at.act_hi(act, b, k, proj[:, k, :], 1.0 if k < QT else rs[:, k : k + 1])

        def pool_prep(pool, b, piece):
            if piece == "x2":
                pool.wait_ge(x_var, b.n + 1)
                nc.gpsimd.tensor_tensor(rstd[:, 0, :], mv[:, 0, :, 1], shared.neghalf[:, 0:QT], ALU.pow).then_inc(x_rstd, 1)
            elif piece == "P3":
                pool.wait_ge(sq_made, 4 * b.n + 4)
                pool.sem_inc(pool_held, 1)
                nc.gpsimd.tensor_scalar(ss[:, :], ss[:, :], 1.0 / H, RMS_EPS, ALU.mult, ALU.add).then_inc(rms_step, 1)
                pool.wait_ge(rms_step, 2 * b.n + 1)
                nc.gpsimd.tensor_tensor(rs[:, :], ss[:, :], shared.neghalf[:, :], ALU.pow).then_inc(rms_step, 1)
                pool.wait_ge(rms_step, 2 * b.n + 2)
                nc.gpsimd.tensor_tensor(rs[:, :], rs[:, :], sc4[:, :], ALU.mult).then_inc(rms_ready, 1)

        K_PREP = 6 + 4

        def dve_prep_(dve, b, piece, chain):
            v = nc.vector
            k = int(piece[1]) if piece[1:].isdigit() else 0
            if piece == "x2":
                chain.batch(b.n)
                dve.wait_ge(acc_in, 32 * b.n + 32)
                chain.link(v.tensor_tensor(accb[:, 0, :, :], accb[:, 0, :, :], accb[:, 1, :, :], ALU.add))
                xb = xs[:, bass.ds(QT * b.n, QT), :]
                chain.link(v.scalar_tensor_tensor(xb, accb[:, 0, :, :], gates[:, 2:3], xb, ALU.mult, ALU.add))
                dve.sem_inc(dve_held, 1)
                for t in range(QT):
                    chain.mark(v.bn_stats(st6[:, 0, t, :], mine(b, t)))
                chain.settle()
                dve.sem_inc(dve_held, 1)
                for t in range(QT):
                    chain.mark(v.bn_aggr(mv[:, 0, t, :], st6[:, 0, t, :]))
                chain.settle()
                v.tensor_scalar(mv[:, 0, :, 1], mv[:, 0, :, 1], LN_EPS, None, ALU.add).then_inc(x_var, 1)
            elif piece == "xn":
                dve.wait_ge(x_rstd, b.n + 1)
                for t in range(QT):
                    last = v.tensor_scalar(xn[:, t, :], mine(b, t), mv[:, 0, t, 0:1], rstd[:, 0, t : t + 1], ALU.subtract, ALU.mult)
                last.then_inc(xn_ready, 1)
            elif piece in ("sq", "sc"):
                for j in range(QT) if piece == "sq" else range(QT, 2 * QT):
                    dve.wait_ge(half_hi, 4 * b.n + j + 1)
                    v.scalar_tensor_tensor(halves[:, j, 1, :], source(j), SC_N if j < QT else SC_C, halves[:, j, 0, :],
                                           ALU.mult, ALU.subtract).then_inc(half_ready, 1)
            elif piece[0] == "P":
                dve.wait_ge(pj_ps, 6 * b.n + k + 1)
                dst = proj[:, k, :] if k < 4 else vbuf[:, b.par, k - 4, :]
                v.scalar_tensor_tensor(dst, bProj[:, :], 1.0 / ((SC_N if k < QT else SC_C) * SC_W), vec[:, k // 2, :],
                                       ALU.mult, ALU.add).then_inc(pj_read, 1)
            elif piece == "r":
                dve.wait_ge(rms_ready, b.n + 1)
                dve.wait_ge(pj_read, 6 * b.n + 4)
                for t in range(QT):
                    v.scalar_tensor_tensor(proj[:, t, :], proj[:, t, :], rs[:, t : t + 1], vec[:, G_Q, :], ALU.mult, ALU.mult)\
                      .then_inc(q_ready, 1)
            elif piece[0] == "h":
                at.dve_lo(dve, b, k, proj[:, k, :], 1.0 if k < QT else rs[:, k : k + 1], chain)
                if k == 3:
                    chain.end("prep1")
            elif piece[0] == "S":
                at.dve_stack(dve, b, k)

        def pe_post(pe, b, piece):
            if piece not in USES:
                return
            k, t = USES.index(piece), int(piece[1])
            before = USES[k - 1]
            if before in COPIED:
                pe.wait_ge(po_copied, 4 * b.n + COPIED.index(before) + 1)
            else:
                pe.wait_ge(po_read, 6 * b.n + 1 + (READ.index(before) + 1 if k else 0))
            if piece[0] == "a":
                pe.wait_ge(at.out_read, 2 * b.n + t + 2)
                for c in range(HC):
                    last = nc.tensor.transpose(bPost[:, c * P : (c + 1) * P], at.outT[:, b.par, t, c * P : (c + 1) * P], shared.id32[:])
            elif piece[0] in "cg":
                pe.wait_ge(a_lo, 4 * b.n + t + (1 if piece[0] == "c" else 3))
                last = turn16(bPost, a16[:, t, :, :])
            else:
                pe.wait_ge(po_copied, 4 * b.n + t + (1 if piece[0] == "d" else 3))
                last = products(bPost[:, :], aT[:, t, :], 3 if piece[0] == "d" else 4)
            last.then_inc(po_ps, 1)

        def act_post(act, b, piece):
            t = int(piece[1]) if piece[1:] else 0
            if piece[0] in "bf":
                act.wait_ge(a_ready, 4 * b.n + t + (1 if piece[0] == "b" else 3))
                nc.scalar.activation(a16[:, t, 0, :], att[:, t, :], ACT.Copy, scale=SC_A if piece[0] == "b" else SC_N).then_inc(a_hi, 1)
            elif piece in COPIED:
                act.wait_ge(po_ps, 10 * b.n + USES.index(piece) + 1)
                nc.scalar.activation(aT[:, t, :], bPost[:, :].bitcast(F16), ACT.Copy).then_inc(po_copied, 1)

        def pool_post(pool, b, piece):
            if piece == "d1":
                pool.wait_ge(p_var, b.n + 1)
                nc.gpsimd.tensor_tensor(rstd[:, 1, :], mv[:, 1, :, 1], shared.neghalf[:, 0:QT], ALU.pow).then_inc(p_rstd, 1)

        K_POST = 1 + 3 * QT + 0

        def dve_post_(dve, b, piece, chain):
            v = nc.vector
            t = int(piece[1]) if piece[1:] else 0
            if piece[0] == "a":
                if t == 0:
                    chain.batch(b.n)
                    dve.wait_ge(at.probs_made, STEPS * b.n + STEPS)
                    chain.link(v.reciprocal(rsum[:, :, :], at.sums[:, b.par, :, :]))
                dve.wait_ge(po_ps, 10 * b.n + t + 1)
                v.tensor_tensor(att[:, t, :].rearrange("p (h d) -> p h d", d=D), bPost[:, :].rearrange("p (h d) -> p h d", d=D),
                                rep(rsum[:, t, :], D, 2), ALU.mult).then_inc(po_read, 1)
                dve.wait_ge(po_read, 6 * b.n + t + 2)
                dve.sem_inc(a_ready, 1)
            elif piece[0] in "bf":
                n = 4 * b.n + t + (1 if piece[0] == "b" else 3)
                dve.wait_ge(a_hi, n)
                v.scalar_tensor_tensor(a16[:, t, 1, :], att[:, t, :], SC_A if piece[0] == "b" else SC_N, a16[:, t, 0, :],
                                       ALU.mult, ALU.subtract).then_inc(a_lo, 1)
            elif piece[0] == "d":
                dve.wait_ge(po_ps, 10 * b.n + 5 + t)
                v.scalar_tensor_tensor(att[:, t, :], bPost[:, :], 1.0 / (SC_A * SC_W), vec[:, B_O, :], ALU.mult, ALU.add).then_inc(po_read, 1)
                dve.wait_ge(po_read, 6 * b.n + 4 + t)
                chain.link(v.scalar_tensor_tensor(mine(b, t), att[:, t, :], gates[:, 1:2], mine(b, t), ALU.mult, ALU.add))
                dve.sem_inc(dve_held, 1)
                chain.link(v.bn_stats(st6[:, 1, t, :], mine(b, t)))
                dve.sem_inc(dve_held, 1)
                chain.link(v.bn_aggr(mv[:, 1, t, :], st6[:, 1, t, :]))
                if t == QT - 1:
                    v.tensor_scalar(mv[:, 1, :, 1], mv[:, 1, :, 1], LN_EPS, None, ALU.add).then_inc(p_var, 1)
            elif piece == "e":
                dve.wait_ge(p_rstd, b.n + 1)
                for t in range(QT):
                    v.tensor_scalar(att[:, t, :], mine(b, t), mv[:, 1, t, 0:1], rstd[:, 1, t : t + 1], ALU.subtract, ALU.mult)\
                     .then_inc(a_ready, 1)
            elif piece[0] == "h":
                dve.wait_ge(po_ps, 10 * b.n + 9 + t)
                dve.wait_ge(out_free, 2 * b.n + 1)
                v.scalar_tensor_tensor(outb[:, t, :], bPost[:, :], 1.0 / (SC_N * SC_W), vec[:, B_T, :], ALU.mult, ALU.add).then_inc(po_read, 1)
                dve.wait_ge(po_read, 6 * b.n + 6 + t)
                v.scalar_tensor_tensor(outb[:, t, :], outb[:, t, :], gates[:, 3:4], mine(b, t), ALU.mult, ALU.add).then_inc(out_ready, 1)
                if t == QT - 1:
                    chain.end("post1")

        @block.sync
        def _(sp):
            for m in range(4):
                sp.dma_start(raw[:, m, :], mats[m].rearrange("p c h -> p (c h)")).then_inc(mats_in, 16)
            for k in range(7):
                sp.dma_start(vec[:, k, :], broadcast_rows(vecs[k], P)).then_inc(vecs_in, 16)
            sp.dma_start(raw_t.rearrange("p (c h) -> p c h", c=HC), ternary.rearrange("(c p) h -> p c h", p=P)).then_inc(tern_in, 16)
            cv = ctx.rearrange("b (t p) h -> b p t h", p=P)
            ov = out.rearrange("b (t p) h -> b p t h", p=P)
            at_batch = lambda v, b: v[b.n] if isinstance(b.n, int) else v[bass.ds(b.n, 1)].rearrange("a p t h -> p (a t) h")

            def load(b):
                for i in range(2):
                    src = shared.acc[i][bass.ds(QT * P * b.n, QT * P), :].rearrange("(t p) h -> p t h", p=P)
                    sp.dma_start(accb[:, i, :, :], src).then_inc(acc_in, 16)
                sp.dma_start(cbuf[:, :, :], at_batch(cv, b)).then_inc(ctx_in, 16)

            def store(b):
                sp.wait_ge(out_ready, 2 * b.n + 2)
                sp.dma_start(at_batch(ov, b), outb[:, :, :]).then_inc(out_stored, 16)
                sp.wait_ge(out_stored, 16 * b.n + 16)
                sp.sem_inc(out_free, 2)

            def load_next(b):
                sp.wait_ge(at.parts_ready, 4 * b.n + 4)
                load(b.next())

            sp.sem_inc(out_free, 1)
            load(Batch(0, 0, 0))
            load_next(Batch(0, 0, 0))

            def body(b):
                load_next(b)
                store(b.prev())

            over_batches(sp, lambda b: None, body, lambda b: store(b.prev()))
            store(Batch(B - 1, 1, (B - 1) // 2))

        @block.gpsimd
        def _(pool):
            nc.gpsimd.memset(sc4[:, 0:QT], SC_Q).then_inc(sc_made, 1)
            nc.gpsimd.memset(sc4[:, QT:4], SC_K).then_inc(sc_made, 1)
            pool.wait_ge(sc_made, 2)
            b0 = Batch(0, 0, 0)
            for piece in all_pieces(PREP):
                pool_prep(pool, b0, piece)

            def body(b, prep, post):
                for s in range(STEPS):
                    for piece in pieces(POST, s) if post else []:
                        pool_post(pool, b.prev(), piece)
                    for piece in pieces(PREP, s) if prep else []:
                        pool_prep(pool, b.next(), piece)

            over_batches(pool, lambda b: body(b, True, False), lambda b: body(b, True, True), lambda b: body(b, False, True))
            for piece in all_pieces(POST):
                pool_post(pool, Batch(B - 1, 1, (B - 1) // 2), piece)

        @block.scalar
        def _(act):
            nc.scalar.preload_act_table(ACT.Exp)
            act.wait_ge(mats_in, 64)
            for m in range(4):
                nc.scalar.activation(w_hi[:, m, :], raw[:, m, :], ACT.Copy, scale=SC_W).then_inc(mat_hi, 1)
            act.wait_ge(tern_in, 16)
            for c in range(HC):
                nc.scalar.activation(junk[:, :], raw_t[:, c * H : (c + 1) * H], ACT.Abs, accum_out=absum[:, c : c + 1]).then_inc(abs_made, 1)
                act.wait_ge(abs_made, c + 1)
            b0 = Batch(0, 0, 0)
            for piece in all_pieces(PREP):
                act_prep(act, b0, piece)
            at.act_exp(act, b0, 0)

            def body(b, prep, post, more):
                for s in range(STEPS):
                    at.act_step(act, b, s, more)
                    for piece in pieces(POST, s) if post else []:
                        act_post(act, b.prev(), piece)
                    for piece in pieces(PREP, s) if prep else []:
                        act_prep(act, b.next(), piece)

            over_batches(act, lambda b: body(b, True, False, True), lambda b: body(b, True, True, True),
                         lambda b: body(b, False, True, False))
            for piece in all_pieces(POST):
                act_post(act, Batch(B - 1, 1, (B - 1) // 2), piece)

        @block.vector
        def _(dve):
            v = nc.vector
            prep, post, ternary_chain = Chain(dve, dve_prep, K_PREP), Chain(dve, dve_post, K_POST), Chain(dve, tern, 0)
            dve.sem_inc(at.stack_ready, 1)
            dve.sem_inc(at.out_read, 1)
            dve.sem_inc(po_read, 1)
            dve.wait_ge(vecs_in, 16 * 7)
            v.tensor_tensor(vec[:, G_Q, :], vec[:, G_Q, :], vec[:, G_K, :], ALU.mult).then_inc(g_made, 1)
            for m in range(4):
                dve.wait_ge(mat_hi, m + 1)
                v.scalar_tensor_tensor(w_lo[:, m, :], raw[:, m, :], SC_W, w_hi[:, m, :], ALU.mult, ALU.subtract).then_inc(mat_lo, 1)
            dve.wait_ge(g_made, 1)
            c, full = ternary_chain, w_hi[:, 4, :]
            q, t1 = raw_t, raw[:, 0, :]
            dve.wait_ge(mat_lo, 4)
            dve.wait_ge(abs_ps, 1)
            c.link(v.tensor_reduce(mean[:, 0:1], bProj[:, 0:HC], AX, ALU.add))
            c.link(v.tensor_scalar(mean[:, 0:1], mean[:, 0:1], 1.0 / (H * H), None, ALU.mult))
            c.link(v.tensor_scalar(mean[:, 1:2], mean[:, 0:1], TERN_EPS, None, ALU.add))
            c.link(v.reciprocal(inv[:, :], mean[:, 1:2]))
            c.link(v.tensor_scalar(t1, q, inv[:, 0:1], ROUND, ALU.mult, ALU.add))
            c.link(v.tensor_scalar(t1, t1, -ROUND, 1.0, ALU.add, ALU.min))
            c.link(v.tensor_scalar(t1, t1, -1.0, mean[:, 0:1], ALU.max, ALU.mult))
            c.link(v.tensor_tensor(t1, t1, q, ALU.subtract))
            c.link(v.tensor_tensor(t1, t1, q, ALU.add))
            c.link(v.tensor_scalar(w_hi[:, 4, :], t1, SC_W, None, ALU.mult))
            c.link(v.scalar_tensor_tensor(w_lo[:, 4, :], t1, SC_W, w_hi[:, 4, :], ALU.mult, ALU.subtract))
            b0 = Batch(0, 0, 0)
            for piece in all_pieces(PREP):
                dve_prep_(dve, b0, piece, prep)
            at.dve_max(dve, b0, 0)
            at.dve_max(dve, b0, 1)

            def body(b, do_prep, do_post, more):
                for s in range(STEPS):
                    at.dve_step(dve, b, s, more, before=do_post)
                    for piece in pieces(POST, s) if do_post else []:
                        dve_post_(dve, b.prev(), piece, post)
                    for piece in pieces(PREP, s) if do_prep else []:
                        dve_prep_(dve, b.next(), piece, prep)

            over_batches(dve, lambda b: body(b, True, False, True), lambda b: body(b, True, True, True),
                         lambda b: body(b, False, True, False))
            end = Batch(B - 1, 1, (B - 1) // 2)
            at.dve_out(dve, end, 1)
            for piece in all_pieces(POST):
                dve_post_(dve, end, piece, post)

        @block.tensor
        def _(pe):
            pe.sem_inc(at.stack_ps, 8)
            pe.wait_ge(abs_made, HC)
            nc.tensor.matmul(bProj[:, 0:HC], shared.ones32[:, :], absum[:, :], start=True, stop=True).then_inc(abs_ps, 1)
            pe.wait_ge(mat_lo, 4)
            pe.wait_ge(tern, 11)
            b0 = Batch(0, 0, 0)
            for piece in all_pieces(PREP):
                pe_prep(pe, b0, piece)
            pe.wait_ge(at.stack_ready, 9)
            at.pe_scores(b0, 0)
            at.pe_scores(b0, 1)

            def body(b, prep, post, more):
                for s in range(STEPS):
                    at.pe_step(pe, b, s, more, before=post)
                    for piece in pieces(POST, s) if post else []:
                        pe_post(pe, b.prev(), piece)
                    for piece in pieces(PREP, s) if prep else []:
                        pe_prep(pe, b.next(), piece)

            over_batches(pe, lambda b: body(b, True, False, True), lambda b: body(b, True, True, True),
                         lambda b: body(b, False, True, False))
            end = Batch(B - 1, 1, (B - 1) // 2)
            at.pe_pv(pe, end, STEPS - 1)
            for piece in all_pieces(POST):
                pe_post(pe, end, piece)


def flamingo(nc, x, ctx, g_xattn, g_ffn, gate_w, w_experts, mats, vecs, ternary, out):
    with ExitStack() as es:
        shared = Shared(nc, es)
        layer0(nc, shared, x, ctx, g_xattn, g_ffn, gate_w)
        experts(nc, shared, w_experts)
        layer1(nc, shared, ctx, mats, vecs, ternary, out)


def arrange(inputs):
    f = {k: np.asarray(v) for k, v in inputs.items()}
    wg, wu, wd = f["L0_ffn_w_gate"], f["L0_ffn_w_up"], f["L0_ffn_w_down"]
    gu = np.concatenate([wg.reshape(E, HC, P, FI), wu.reshape(E, HC, P, FI)], axis=3)
    gu = gu.transpose(0, 2, 1, 3).reshape(E, P, HC * GU)
    rest = np.concatenate([wd[:, P:FI], wd[:, P:FI]], axis=1)
    experts = np.concatenate([gu, wd[:, 0:P], rest], axis=2)
    mats = np.stack([f["L1_xattn_w_q"].T, f["L1_xattn_w_k_img"].T, f["L1_xattn_w_v_img"].T, f["L1_xattn_w_o"].T])
    vecs = np.stack([f["L1_xattn_b_q"], f["L1_xattn_b_k_img"], f["L1_xattn_b_v_img"], f["L1_xattn_b_o"],
                     f["L1_ffn_bias"], f["L1_xattn_g_q"], f["L1_xattn_g_k_img"]])
    return {
        "x": f["x"], "ctx": f["ctx_2048"], "g_xattn": f["g_xattn"], "g_ffn": f["g_ffn"], "gate_w": f["L0_ffn_gate_w"],
        "experts": experts, "mats": mats.reshape(4, HC, P, H).transpose(0, 2, 1, 3), "vecs": vecs,
        "ternary": np.ascontiguousarray(f["L1_ffn_weight"].T),
    }


def kernel(**inputs):
    import numpy as _np
    import concourse.bacc as _bacc
    from concourse import mybir as _mybir
    from concourse.bass_utils import run_bass_kernel_spmd as _run

    nc = _bacc.Bacc("TRN2", target_bir_lowering=False, num_devices=1)
    arrays, args = {}, []
    for name, a in arrange(inputs).items():
        arrays[f"in_{name}_dram"] = _np.ascontiguousarray(a)
        args.append(nc.dram_tensor(f"in_{name}_dram", a.shape, _mybir.dt.from_np(a.dtype), kind="ExternalInput").ap())
    args.append(nc.dram_tensor("out_0_dram", (B, S, H), F32, kind="ExternalOutput").ap())
    flamingo(nc, *args)
    r = _run(nc, [arrays], core_ids=[0])
    return r.results[0]["out_0_dram"]
```
